# Optimizing a Trainium2 kernel written in Bass

```python
import numpy as np
import jax
import jax.numpy as jnp

def _softmax(x, axis=-1):
    return jax.nn.softmax(x, axis=axis)

def _gelu(x):
    return jax.nn.gelu(x, approximate=True)

def _silu(x):
    return jax.nn.silu(x)

def _sigmoid(x):
    return jax.nn.sigmoid(x)

def _layernorm(x, axis=-1, eps=1e-05):
    m = jnp.mean(x, axis=axis, keepdims=True)
    v = jnp.var(x, axis=axis, keepdims=True)
    return (x - m) / jnp.sqrt(v + eps)

def _scatter_add(tgt, idx, src, axis=0):
    return tgt.at[idx].add(src)

def _segment_sum(src, seg, n):
    return jax.ops.segment_sum(src, seg, n)
kernel_name = 'mk_perceiver_d1_seqx_r4_14decc'

def setup_inputs(seed: int=0):
    np.random.seed(seed)
    _w = jnp.asarray

    def _rec_inputs():
        import jax
        import jax.numpy as jnp
        _rk = jax.random.key(seed)
        x = -0.0002928 + 1 * jax.random.normal(jax.random.fold_in(_rk, 1), (32, 32, 512), jnp.float32)
        _lenS = 32 - jax.random.randint(jax.random.fold_in(_rk, 7), (32,), 0, max(1, 32 // 4) + 1, jnp.int32)
        _lenS2 = 257 - jax.random.randint(jax.random.fold_in(_rk, 8), (32,), 0, max(1, 257 // 4) + 1, jnp.int32)
        _ctx_512P = jax.random.normal(jax.random.fold_in(_rk, 11), (32, 16, 128), jnp.float32)
        _ctx_512c = jax.random.dirichlet(jax.random.fold_in(_rk, 511), 0.3 * jnp.ones((16,), jnp.float32), (32, 257))
        _ctx_512t = jnp.einsum('bsk,bkd->bsd', _ctx_512c, _ctx_512P)
        _ctx_512t = _ctx_512t * jax.lax.rsqrt(jnp.mean(jnp.square(_ctx_512t)) + 1e-12) * 0.953939
        ctx_512 = 0.000227908 + 0.99994 * (_ctx_512t + 0.3 * jax.random.normal(jax.random.fold_in(_rk, 611), (32, 257, 128), jnp.float32))
        return (x, ctx_512)
    x, ctx_512 = _rec_inputs()

    def _L0_xattn_setup():
        import jax, jax.numpy as jnp
        import numpy as np
        B, S, L = (2, 256, 256)
        DIM_Q, H, K, D_C, D_CQ, R = (512, 16, 128, 128, 384, 64)

        def _rope_tables(seq_len, dim, dtype):
            inv_freq = 1.0 / 10000.0 ** (jnp.arange(0, dim, 2, dtype=dtype) / dim)
            t = jnp.arange(seq_len, dtype=dtype)
            freqs = t[:, None] * inv_freq[None, :]
            sin = jnp.repeat(jnp.sin(freqs), 2, axis=-1)
            cos = jnp.repeat(jnp.cos(freqs), 2, axis=-1)
            return (sin, cos)

        def _rotate_half(x):
            h = x.shape[-1] // 2
            return jnp.concatenate([-x[..., h:], x[..., :h]], axis=-1)
        key = jax.random.key(seed)
        ks = jax.random.split(key, 8)
        s_in = 1.0 / np.sqrt(DIM_Q)
        s_k = 1.0 / np.sqrt(K)
        s_cq = 1.0 / np.sqrt(D_CQ)
        s_c = 1.0 / np.sqrt(D_C)
        return {'hidden_q': jax.random.normal(ks[0], (B, S, DIM_Q), jnp.float32), 'kv_c': jax.random.normal(ks[1], (B, L, D_C), jnp.float32), 'Wq': jax.random.normal(ks[2], (H * K, DIM_Q), jnp.float32) * s_in, 'w_kc_q': jax.random.normal(ks[3], (H, K, D_CQ), jnp.float32) * s_k, 'w_kc_kv': jax.random.normal(ks[4], (H, K, D_C), jnp.float32) * s_k, 'W_qr': jax.random.normal(ks[5], (H, D_CQ, R), jnp.float32) * s_cq / np.sqrt(R), 'W_kr': jax.random.normal(ks[6], (H, D_C, R), jnp.float32) * s_c, 'Wo': jax.random.normal(ks[7], (DIM_Q, H * K), jnp.float32) * s_k}
    _L0_xattn_all = _L0_xattn_setup()
    _L0_xattn_in = {k: v for k, v in _L0_xattn_all.items() if k in ('Wq', 'w_kc_q', 'w_kc_kv', 'W_qr', 'W_kr', 'Wo')}
    del _L0_xattn_all

    def _L0_attn_setup():
        import jax, jax.numpy as jnp
        import numpy as np
        N_HEADS = 16
        N_KV_HEADS = 4
        HEAD_DIM = 128
        D_MODEL = 512
        SINK = 4
        WINDOW = 64
        B, T = (2, 512)

        def _sink_window_mask(t: int) -> jnp.ndarray:
            pos = jnp.arange(t)
            q = pos[:, None]
            k = pos[None, :]
            return (k <= q) & ((k < SINK) | (k >= q - WINDOW + 1))

        def _masked_softmax(scores: jnp.ndarray, mask: jnp.ndarray) -> jnp.ndarray:
            floor = jnp.finfo(scores.dtype).min
            ms = jnp.where(mask, scores, floor)
            row_max = jnp.max(ms, axis=-1, keepdims=True)
            row_max = jnp.where(jnp.isfinite(row_max), row_max, jnp.zeros_like(row_max))
            ex = jnp.exp(ms - row_max) * mask.astype(scores.dtype)
            denom = jnp.maximum(jnp.sum(ex, axis=-1, keepdims=True), 1e-09)
            return ex / denom
        key = jax.random.key(seed)
        k0, k1, k2, k3, k4 = jax.random.split(key, 5)
        s = 1.0 / np.sqrt(D_MODEL)
        return {'x': jax.random.normal(k0, (B, T, D_MODEL), dtype=jnp.float32), 'wq': jax.random.normal(k1, (N_HEADS * HEAD_DIM, D_MODEL), dtype=jnp.float32) * s, 'wk': jax.random.normal(k2, (N_KV_HEADS * HEAD_DIM, D_MODEL), dtype=jnp.float32) * s, 'wv': jax.random.normal(k3, (N_KV_HEADS * HEAD_DIM, D_MODEL), dtype=jnp.float32) * s, 'wo': jax.random.normal(k4, (D_MODEL, N_HEADS * HEAD_DIM), dtype=jnp.float32) * s}
    _L0_attn_all = _L0_attn_setup()
    _L0_attn_in = {k: v for k, v in _L0_attn_all.items() if k in ('wq', 'wk', 'wv', 'wo')}
    del _L0_attn_all

    def _L0_ffn_setup():
        import jax, jax.numpy as jnp
        import numpy as np
        B, S, D, M, E, K = (4, 512, 512, 1024, 8, 2)

        def _routed_moe(x, gate_w, w0, w1, wo):
            T = x.shape[0]
            logits = jnp.einsum('td,de->te', x, gate_w)
            top_logits, top_idx = jax.lax.top_k(logits, K)
            top_w = jax.nn.softmax(top_logits, axis=-1)
            cw = jnp.zeros((T, E), dtype=x.dtype).at[jnp.arange(T)[:, None], top_idx].add(top_w)
            out = jnp.zeros_like(x)
            for e in range(E):
                h = jax.nn.silu(x @ w0[e]) * (x @ w1[e])
                out = out + cw[:, e:e + 1] * (h @ wo[e])
            return out
        key = jax.random.key(seed)
        ks = jax.random.split(key, 5)
        inputs = jax.random.normal(ks[0], (B, S, D), dtype=jnp.float32)
        gate_w = jax.random.normal(ks[1], (D, E), dtype=jnp.float32) * D ** (-0.5)
        w0 = jax.random.normal(ks[2], (E, D, M), dtype=jnp.float32) * D ** (-0.5)
        w1 = jax.random.normal(ks[3], (E, D, M), dtype=jnp.float32) * D ** (-0.5)
        wo = jax.random.normal(ks[4], (E, M, D), dtype=jnp.float32) * M ** (-0.5)
        decoder_segment_ids = jax.random.randint(jax.random.fold_in(key, 1), (B, S), 0, 2).astype(jnp.int32)
        decoder_positions = jnp.tile(jnp.arange(S, dtype=jnp.int32)[None, :], (B, 1))
        return {'inputs': inputs, 'gate_w': gate_w, 'w0': w0, 'w1': w1, 'wo': wo, 'decoder_segment_ids': decoder_segment_ids, 'decoder_positions': decoder_positions}
    _L0_ffn_all = _L0_ffn_setup()
    _L0_ffn_in = {k: v for k, v in _L0_ffn_all.items() if k in ('gate_w', 'w0', 'w1', 'wo', 'decoder_segment_ids', 'decoder_positions')}
    del _L0_ffn_all
    return {'x': x, 'ctx_512': ctx_512, 'L0_xattn_Wq': _L0_xattn_in['Wq'], 'L0_xattn_w_kc_q': _L0_xattn_in['w_kc_q'], 'L0_xattn_w_kc_kv': _L0_xattn_in['w_kc_kv'], 'L0_xattn_W_qr': _L0_xattn_in['W_qr'], 'L0_xattn_W_kr': _L0_xattn_in['W_kr'], 'L0_xattn_Wo': _L0_xattn_in['Wo'], 'L0_attn_wq': _L0_attn_in['wq'], 'L0_attn_wk': _L0_attn_in['wk'], 'L0_attn_wv': _L0_attn_in['wv'], 'L0_attn_wo': _L0_attn_in['wo'], 'L0_ffn_gate_w': _L0_ffn_in['gate_w'], 'L0_ffn_w0': _L0_ffn_in['w0'], 'L0_ffn_w1': _L0_ffn_in['w1'], 'L0_ffn_wo': _L0_ffn_in['wo'], 'L0_ffn_decoder_segment_ids': _L0_ffn_in['decoder_segment_ids'], 'L0_ffn_decoder_positions': _L0_ffn_in['decoder_positions']}

def reference(x, ctx_512, L0_xattn_Wq, L0_xattn_w_kc_q, L0_xattn_w_kc_kv, L0_xattn_W_qr, L0_xattn_W_kr, L0_xattn_Wo, L0_attn_wq, L0_attn_wk, L0_attn_wv, L0_attn_wo, L0_ffn_gate_w, L0_ffn_w0, L0_ffn_w1, L0_ffn_wo, L0_ffn_decoder_segment_ids, L0_ffn_decoder_positions):
    import jax
    import jax.numpy as jnp

    def _L0_xattn_ref(hidden_q, kv_c, Wq, w_kc_q, w_kc_kv, W_qr, W_kr, Wo):
        import jax, jax.numpy as jnp
        import numpy as np
        B, S, L = (2, 256, 256)
        DIM_Q, H, K, D_C, D_CQ, R = (512, 16, 128, 128, 384, 64)

        def _rope_tables(seq_len, dim, dtype):
            inv_freq = 1.0 / 10000.0 ** (jnp.arange(0, dim, 2, dtype=dtype) / dim)
            t = jnp.arange(seq_len, dtype=dtype)
            freqs = t[:, None] * inv_freq[None, :]
            sin = jnp.repeat(jnp.sin(freqs), 2, axis=-1)
            cos = jnp.repeat(jnp.cos(freqs), 2, axis=-1)
            return (sin, cos)

        def _rotate_half(x):
            h = x.shape[-1] // 2
            return jnp.concatenate([-x[..., h:], x[..., :h]], axis=-1)
        b, s, _ = hidden_q.shape
        l = kv_c.shape[1]
        q_hk = (hidden_q @ Wq.T).reshape(b, s, H, K)
        q_big = jnp.einsum('bshk,hkq->bshq', q_hk, w_kc_q)
        sin, cos = _rope_tables(l, D_C, kv_c.dtype)
        kv_rope = kv_c * cos[None] + _rotate_half(kv_c) * sin[None]
        q_r = jnp.einsum('bshq,hqr->bhsr', q_big, W_qr)
        k_r = jnp.einsum('bld,hdr->bhlr', kv_rope, W_kr)
        scores = jnp.einsum('bhsr,bhlr->bhsl', q_r, k_r)
        attn = jax.nn.softmax(scores, axis=-1)
        ctx_c = jnp.einsum('bhsl,bld->bhsd', attn, kv_rope)
        ctx_lat = jnp.einsum('bhsd,hkd->bshk', ctx_c, w_kc_kv)
        out = ctx_lat.reshape(b, s, H * K) @ Wo.T
        return out

    def _L0_attn_ref(x, wq, wk, wv, wo):
        import jax, jax.numpy as jnp
        import numpy as np
        N_HEADS = 16
        N_KV_HEADS = 4
        HEAD_DIM = 128
        D_MODEL = 512
        SINK = 4
        WINDOW = 64
        B, T = (2, 512)

        def _sink_window_mask(t: int) -> jnp.ndarray:
            pos = jnp.arange(t)
            q = pos[:, None]
            k = pos[None, :]
            return (k <= q) & ((k < SINK) | (k >= q - WINDOW + 1))

        def _masked_softmax(scores: jnp.ndarray, mask: jnp.ndarray) -> jnp.ndarray:
            floor = jnp.finfo(scores.dtype).min
            ms = jnp.where(mask, scores, floor)
            row_max = jnp.max(ms, axis=-1, keepdims=True)
            row_max = jnp.where(jnp.isfinite(row_max), row_max, jnp.zeros_like(row_max))
            ex = jnp.exp(ms - row_max) * mask.astype(scores.dtype)
            denom = jnp.maximum(jnp.sum(ex, axis=-1, keepdims=True), 1e-09)
            return ex / denom
        b, t, _ = x.shape
        group = N_HEADS // N_KV_HEADS
        q = (x @ wq.T).reshape(b, t, N_HEADS, HEAD_DIM).transpose(0, 2, 1, 3)
        k = (x @ wk.T).reshape(b, t, N_KV_HEADS, HEAD_DIM).transpose(0, 2, 1, 3)
        v = (x @ wv.T).reshape(b, t, N_KV_HEADS, HEAD_DIM).transpose(0, 2, 1, 3)
        k_full = jnp.repeat(k, group, axis=1)
        v_full = jnp.repeat(v, group, axis=1)
        scores = jnp.einsum('bhtd,bhsd->bhts', q, k_full) / np.sqrt(HEAD_DIM)
        mask = _sink_window_mask(t)[None, None, :, :]
        attn = _masked_softmax(scores.astype(jnp.float32), mask).astype(x.dtype)
        out = jnp.einsum('bhts,bhsd->bhtd', attn, v_full)
        out = out.transpose(0, 2, 1, 3).reshape(b, t, N_HEADS * HEAD_DIM)
        return out @ wo.T

    def _L0_ffn_ref(inputs, gate_w, w0, w1, wo, decoder_segment_ids, decoder_positions):
        import jax, jax.numpy as jnp
        import numpy as np
        B, S, D, M, E, K = (4, 512, 512, 1024, 8, 2)

        def _routed_moe(x, gate_w, w0, w1, wo):
            T = x.shape[0]
            logits = jnp.einsum('td,de->te', x, gate_w)
            top_logits, top_idx = jax.lax.top_k(logits, K)
            top_w = jax.nn.softmax(top_logits, axis=-1)
            cw = jnp.zeros((T, E), dtype=x.dtype).at[jnp.arange(T)[:, None], top_idx].add(top_w)
            out = jnp.zeros_like(x)
            for e in range(E):
                h = jax.nn.silu(x @ w0[e]) * (x @ w1[e])
                out = out + cw[:, e:e + 1] * (h @ wo[e])
            return out
        b, s, d = inputs.shape
        x = inputs.reshape(b * s, d)
        out = _routed_moe(x, gate_w, w0, w1, wo)
        return out.reshape(b, s, d)
    x = x + _L0_xattn_ref(_layernorm(x, axis=-1), ctx_512, L0_xattn_Wq, L0_xattn_w_kc_q, L0_xattn_w_kc_kv, L0_xattn_W_qr, L0_xattn_W_kr, L0_xattn_Wo)
    x = x + _L0_attn_ref(_layernorm(x, axis=-1), L0_attn_wq, L0_attn_wk, L0_attn_wv, L0_attn_wo)
    x = x + _L0_ffn_ref(_layernorm(x, axis=-1), L0_ffn_gate_w, L0_ffn_w0, L0_ffn_w1, L0_ffn_wo, L0_ffn_decoder_segment_ids, L0_ffn_decoder_positions)
    return x

_drawn_inputs = setup_inputs


def setup_inputs(seed=0):
    import zlib

    import numpy as np

    out = dict(_drawn_inputs(seed))
    spreads = {}
    factors = {}
    for name, (base, spread) in spreads.items():
        noise = np.random.default_rng([zlib.crc32(name.encode()), seed]).standard_normal(out[name].shape)
        drawn = base * np.exp(spread * noise) if base else spread * noise
        out[name] = jnp.asarray(drawn.astype(out[name].dtype))
    for name, factor in factors.items():
        out[name] = (out[name] * factor).astype(out[name].dtype)
    return out
```

```python
from contextlib import ExitStack


import numpy as np

import concourse.bass as bass
from concourse import mybir

F32 = mybir.dt.float32
F32R = mybir.dt.float32r
I32 = mybir.dt.int32
U32 = mybir.dt.uint32
ALU = mybir.AluOpType
ACT = mybir.ActivationFunctionType
AX = mybir.AxisListType.X

P = 128
B, S, D = 32, 32, 512
L, DC = 257, 128
H, R, DCQ = 16, 64, 384
KVH, G = 4, 4
E, M = 8, 1024
T = B * S
NT = T // P
BT = P // S
DCH = D // P
LC = L // P
LP = L + 1
BANK = 512
EPS = 1e-5
SG = 4
GB = B // SG
GT = T // SG
CAP = 256
MAXSLOT = E + 2 * T // CAP
MASKED = -3.0e38


class Shared:
    pass


def split_lo(nc, out, value, hi):
    return nc.vector.tensor_tensor(out, value, hi.bitcast(F32), ALU.subtract)


def three_passes(nc, out, lhs_hi, lhs_lo, rhs_hi, rhs_lo, first, last):
    nc.tensor.matmul(out, lhs_lo, rhs_hi, start=first, stop=False)
    nc.tensor.matmul(out, lhs_hi, rhs_lo, start=False, stop=False)
    return nc.tensor.matmul(out, lhs_hi, rhs_hi, start=False, stop=last)


def numbered(steps, kinds):
    return {s: n for n, s in enumerate([s for s in steps if s[0] in kinds])}


class LayerNorm:

    def __init__(self, nc, ctx, name):
        def sb(what, shape):
            return ctx.enter_context(nc.sbuf_tensor(f"{name}_{what}", shape, F32))

        self.nc = nc
        self.stats, self.mv = sb("stats", [P, NT, 6]), sb("mv", [P, NT, 2])
        self.var, self.root, self.inv, self.corr, self.rstd = (sb(n, [P, NT]) for n in ("var", "root", "inv", "corr", "rstd"))
        self.stats_done, self.var_done, self.root_done, self.chain = (
            ctx.enter_context(nc.semaphore(f"{name}_{n}")) for n in ("stats_done", "var_done", "root_done", "chain"))
        self.stats_n = self.chain_n = self.ranges = self.roots = 0

    def step(self, dve, instruction):
        instruction.then_inc(self.chain, 1)
        self.chain_n += 1
        dve.wait_ge(self.chain, self.chain_n)

    def statistics(self, dve, x, t):
        self.nc.vector.bn_stats(self.stats[:, t], x).then_inc(self.stats_done, 1)
        self.stats_n += 1

    def variance(self, dve, t0, t1):
        dve.wait_ge(self.stats_done, self.stats_n)
        for t in range(t0, t1):
            last = self.nc.vector.bn_aggr(self.mv[:, t], self.stats[:, t])
        self.step(dve, last)
        self.nc.vector.tensor_scalar_add(self.var[:, t0:t1], self.mv[:, t0:t1, 1], EPS).then_inc(self.var_done, 1)

    def take_root(self, act, t0, t1):
        self.roots += 1
        act.wait_ge(self.var_done, self.roots)
        self.nc.scalar.activation(self.root[:, t0:t1], self.var[:, t0:t1], ACT.Sqrt).then_inc(self.root_done, 1)

    def power(self, dve, t0, t1):
        v, var, inv, corr = self.nc.vector, self.var[:, t0:t1], self.inv[:, t0:t1], self.corr[:, t0:t1]
        self.ranges += 1
        dve.wait_ge(self.root_done, self.ranges)
        self.step(dve, v.reciprocal(inv, self.root[:, t0:t1]))
        self.step(dve, v.tensor_tensor(corr, inv, inv, ALU.mult))
        self.step(dve, v.tensor_tensor(corr, corr, var, ALU.mult))
        self.step(dve, v.tensor_scalar(corr, corr, -0.5, 1.5, ALU.mult, ALU.add))
        self.step(dve, v.tensor_tensor(self.rstd[:, t0:t1], inv, corr, ALU.mult))

    def apply(self, t, out, x):
        return self.nc.vector.tensor_scalar(out, x, self.mv[:, t, 0:1], self.rstd[:, t:t + 1], ALU.subtract, ALU.mult)


def prepare(nc, A, sh):
    HG = 4
    NG = H // HG
    with ExitStack() as ctx:
        def sb(name, shape, dt=F32):
            return ctx.enter_context(nc.sbuf_tensor("p_" + name, shape, dt))

        def sem(name):
            return ctx.enter_context(nc.semaphore("p_" + name))

        x = sb("x", [P, NT, D])
        xn = sb("xn", [P, 2, D])
        ln = LayerNorm(nc, ctx, "p_ln")
        kcq = sb("kcq", [P, 2, HG, DCQ])
        kcqT = sb("kcqT", [P, 2, DCQ // P, HG, P])
        wq = sb("wq", [P, 2, HG, D])
        wqr = sb("wqr", [P, DCQ // P, H, R])
        m2 = sb("m2", [P, 2, HG, R])
        wkr = sb("wkr", [P, H, R])
        last = sb("last", [B, DC])
        last_cos, last_sin = sb("last_cos", [B, DC]), sb("last_sin", [B, DC])
        last_rot = sb("last_rot", [B, DC])
        last_a, last_b = sb("last_a", [B, DC]), sb("last_b", [B, DC])
        NB = 8
        ring = [ctx.enter_context(nc.psum_tensor(f"p_ring{n}", [P, BANK], F32)) for n in range(NB)]

        ident_in, x_in, wqr_in, wkr_in, last_in = (sem(n) for n in ("ident_in", "x_in", "wqr_in", "wkr_in", "last_in"))
        kcq_in, wq_in = [sem("kcq_in0"), sem("kcq_in1")], [sem("wq_in0"), sem("wq_in1")]
        ready, hi_done, free = sem("ready"), sem("hi"), sem("free")
        zeroed = sem("zeroed")
        xn_done, dve_chain, last_done, last_out = sem("xn_done"), sem("dve_chain"), sem("last_done"), sem("last_out")

        steps = [("kcqT", 0, q) for q in range(3)] + [("xT", 0), ("m2", 0), ("xT", 1)]
        for g in range(1, NG):
            steps += [("kcqT", g, q) for q in range(3)] + [("m1", g - 1, c) for c in range(2)]
            steps += [("m2", g), ("xT", 2 * g), ("xT", 2 * g + 1)]
        steps += [("krT", 0), ("krT", 1), ("lastT",), ("m1", NG - 1, 0), ("m1", NG - 1, 1)]
        job = {s: n for n, s in enumerate(steps)}
        split = numbered(steps, ("xT", "m1", "krT", "lastT"))
        xs = [s for s in steps if s[0] == "xT"]

        with nc.Block() as block:
            @block.sync
            def _(sp):
                sp.dma_start(sh.ident[:, :], A["ident"]).then_inc(ident_in, 16)
                kcq_d = A["w_kc_q"].rearrange("(g h) k q -> g k h q", h=HG)
                wq_d = A["Wq"].rearrange("(g h k) d -> g k h d", h=HG, k=P)
                x_d = A["x"].rearrange("b s d -> (b s) d").rearrange("(n p) d -> p n d", p=P)
                sp.dma_start(kcq[:, 0], kcq_d[0]).then_inc(kcq_in[0], 16)
                sp.dma_start(x[:, 0:NT // 2], x_d[:, 0:NT // 2]).then_inc(x_in, 16)
                sp.dma_start(kcq[:, 1], kcq_d[1]).then_inc(kcq_in[1], 16)
                sp.dma_start(wq[:, 0], wq_d[0]).then_inc(wq_in[0], 16)
                sp.wait_ge(x_in, 16)
                sp.dma_start(x[:, NT // 2:], x_d[:, NT // 2:]).then_inc(x_in, 16)
                sp.dma_start(wq[:, 1], wq_d[1]).then_inc(wq_in[1], 16)
                for g in range(2, NG):
                    sp.wait_ge(ready, job["kcqT", g - 2, 2] + 1)
                    sp.dma_start(kcq[:, g % 2], kcq_d[g]).then_inc(kcq_in[g % 2], 16)
                    sp.wait_ge(ready, job["m1", g - 2, 1] + 1)
                    sp.dma_start(wq[:, g % 2], wq_d[g]).then_inc(wq_in[g % 2], 16)
                sp.wait_ge(last_done, 1)
                sp.dma_start(sh.last_dram, last_rot[:, :]).then_inc(last_out, 16)
                sp.wait_ge(last_out, 16)

            @block.gpsimd
            def _(pool):
                nc.gpsimd.memset(sh.krT_hi[:, :, :].bitcast(F32), 0.0).then_inc(zeroed, 1)
                nc.gpsimd.memset(sh.krT_lo[:, :, :].bitcast(F32), 0.0).then_inc(zeroed, 1)

            @block.scalar
            def _(act):
                for c in range(DCQ // P):
                    act.dma_start(wqr[:, c], A["W_qr"][:, c * P:(c + 1) * P, :].rearrange("h q r -> q h r")).then_inc(wqr_in, 16)
                act.dma_start(last[:, :], A["ctx"][:, L - 1, :]).then_inc(last_in, 16)
                act.dma_start(last_cos[:, :], A["last_cos"]).then_inc(last_in, 16)
                act.dma_start(last_sin[:, :], A["last_sin"]).then_inc(last_in, 16)
                act.dma_start(wkr[:, :, :], A["W_kr"].rearrange("h c r -> c h r")).then_inc(wkr_in, 16)
                ln.take_root(act, 0, NT // 2)
                for s in steps:
                    if s not in split:
                        continue
                    if s == ("xT", 2):
                        ln.take_root(act, NT // 2, NT)
                    n = job[s]
                    bank = ring[n % NB]
                    act.wait_ge(ready, n + 1)
                    if s[0] == "xT":
                        out = sh.xT_hi[:, :, s[1] * P:(s[1] + 1) * P]
                        nc.scalar.copy(out, bank[:, :].rearrange("p (c t) -> p c t", c=DCH)).then_inc(hi_done, 1)
                    elif s[0] == "m1":
                        _, g, c = s
                        out = sh.m1_hi[:, 2 * c:2 * c + 2, g * HG * R:(g + 1) * HG * R]
                        nc.scalar.copy(out, bank[:, :].rearrange("p (c r) -> p c r", c=2)).then_inc(hi_done, 1)
                    elif s[0] == "krT":
                        act.wait_ge(zeroed, 2)
                        for e in range(2):
                            rows, heads = slice(R * e, R * e + R), slice(8 * s[1] + e, 8 * s[1] + 8, 2)
                            cp = nc.scalar.copy(sh.krT_hi[rows, heads, :], bank[rows, :].rearrange("p (j c) -> p j c", j=4))
                        cp.then_inc(hi_done, 1)
                    else:
                        nc.scalar.copy(sh.lastT_hi[:, :], bank[:, 0:B]).then_inc(hi_done, 1)

            @block.vector
            def _(dve):
                dve.wait_ge(last_in, 48)
                nc.vector.tensor_tensor(last_a[:, :], last[:, :], last_cos[:, :], ALU.mult).then_inc(dve_chain, 1)
                nc.vector.tensor_tensor(last_b[:, 0:64], last[:, 64:128], last_sin[:, 0:64], ALU.mult).then_inc(dve_chain, 1)
                nc.vector.tensor_tensor(last_b[:, 64:128], last[:, 0:64], last_sin[:, 64:128], ALU.mult).then_inc(dve_chain, 1)
                dve.wait_ge(dve_chain, 3)
                nc.vector.tensor_tensor(last_rot[:, :], last_a[:, :], last_b[:, :], ALU.add).then_inc(last_done, 1)

                def norm_range(t0, t1):
                    dve.wait_ge(x_in, 16 * t1 // (NT // 2))
                    for t in range(t0, t1):
                        ln.statistics(dve, x[:, t], t)
                    ln.variance(dve, t0, t1)
                    ln.power(dve, t0, t1)

                def norm(t):
                    if t >= 2:
                        dve.wait_ge(ready, job["xT", t - 2] + 1)
                    ln.apply(t, xn[:, t % 2], x[:, t]).then_inc(xn_done, 1)

                norm_range(0, NT // 2)
                norm(0)
                norm(1)
                for s in steps:
                    n = job[s]
                    bank = ring[n % NB]
                    if s in split:
                        dve.wait_ge(hi_done, split[s] + 1)
                    else:
                        dve.wait_ge(ready, n + 1)
                    if s[0] == "kcqT":
                        _, g, q = s
                        nc.vector.tensor_copy(kcqT[:, g % 2, q].rearrange("p h k -> p (h k)"), bank[:, :]).then_inc(free, 1)
                    elif s[0] == "m2":
                        g = s[1]
                        nc.vector.tensor_copy(m2[:, g % 2].rearrange("p h r -> p (h r)"), bank[:, 0:HG * R]).then_inc(free, 1)
                    elif s[0] == "xT":
                        at = slice(s[1] * P, (s[1] + 1) * P)
                        split_lo(nc, sh.xT_lo[:, :, at], bank[:, :].rearrange("p (c t) -> p c t", c=DCH), sh.xT_hi[:, :, at]).then_inc(free, 1)
                        if s[1] == 1:
                            norm_range(NT // 2, NT)
                        if s[1] + 2 < NT:
                            norm(s[1] + 2)
                    elif s[0] == "m1":
                        _, g, c = s
                        at = slice(g * HG * R, (g + 1) * HG * R)
                        split_lo(nc, sh.m1_lo[:, 2 * c:2 * c + 2, at], bank[:, :].rearrange("p (c r) -> p c r", c=2),
                                 sh.m1_hi[:, 2 * c:2 * c + 2, at]).then_inc(free, 1)
                    elif s[0] == "krT":
                        for e in range(2):
                            rows, heads = slice(R * e, R * e + R), slice(8 * s[1] + e, 8 * s[1] + 8, 2)
                            lo = split_lo(nc, sh.krT_lo[rows, heads, :], bank[rows, :].rearrange("p (j c) -> p j c", j=4), sh.krT_hi[rows, heads, :])
                        lo.then_inc(free, 1)
                    else:
                        split_lo(nc, sh.lastT_lo[:, :], bank[:, 0:B], sh.lastT_hi[:, :]).then_inc(free, 1)

            @block.tensor
            def _(pe):
                pe.wait_ge(ident_in, 16)
                for s in steps:
                    n = job[s]
                    bank = ring[n % NB]
                    if n >= NB:
                        pe.wait_ge(free, n - NB + 1)
                    if s[0] == "kcqT":
                        _, g, q = s
                        pe.wait_ge(kcq_in[g % 2], 16 * (g // 2 + 1))
                        for h in range(HG):
                            mm = nc.tensor.transpose(bank[:, h * P:(h + 1) * P], kcq[:, g % 2, h, q * P:(q + 1) * P], sh.ident[:, :])
                    elif s[0] == "m2":
                        g = s[1]
                        pe.wait_ge(wqr_in, 48)
                        pe.wait_ge(free, job["kcqT", g, 2] + 1)
                        for h in range(HG):
                            for q in range(3):
                                mm = nc.tensor.matmul(bank[:, h * R:(h + 1) * R], kcqT[:, g % 2, q, h, :], wqr[:, q, g * HG + h, :],
                                                      start=q == 0, stop=q == 2)
                    elif s[0] == "m1":
                        _, g, c = s
                        pe.wait_ge(wq_in[g % 2], 16 * (g // 2 + 1))
                        pe.wait_ge(free, job["m2", g] + 1)
                        for cc in range(2):
                            for h in range(HG):
                                mm = nc.tensor.matmul(bank[:, (cc * HG + h) * R:(cc * HG + h + 1) * R],
                                                      wq[:, g % 2, h, (2 * c + cc) * P:(2 * c + cc + 1) * P], m2[:, g % 2, h, :],
                                                      start=True, stop=True)
                    elif s[0] == "xT":
                        pe.wait_ge(xn_done, s[1] + 1)
                        for c in range(DCH):
                            mm = nc.tensor.transpose(bank[:, c * P:(c + 1) * P], xn[:, s[1] % 2, c * P:(c + 1) * P], sh.ident[:, :])
                    elif s[0] == "krT":
                        pe.wait_ge(wkr_in, 16)
                        for j in range(4):
                            h = 2 * (4 * s[1] + j)
                            mm = nc.tensor.transpose(bank[:, j * P:(j + 1) * P], wkr[:, h:h + 2, :].rearrange("p h r -> p (h r)"), sh.ident[:, :])
                    else:
                        pe.wait_ge(last_done, 1)
                        mm = nc.tensor.transpose(bank[:, 0:B], last_rot[:, :], sh.ident[0:B, 0:B])
                    mm.then_inc(ready, 1)


def cross_attention(nc, A, sh):
    with ExitStack() as ctx:
        def sb(name, shape, dt=F32):
            return ctx.enter_context(nc.sbuf_tensor("x_" + name, shape, dt))

        def sem(name):
            return ctx.enter_context(nc.semaphore("x_" + name))

        NQ = 4
        PAIRS = H // 2
        cos, sin = sb("cos", [P, LC, DC]), sb("sin", [P, LC, DC])
        qr_hi, qr_lo = sb("qr_hi", [P, NQ, GT], F32R), sb("qr_lo", [P, NQ, GT], F32R)
        qp_hi, qp_lo = sb("qp_hi", [P, GB, H, S], F32R), sb("qp_lo", [P, GB, H, S], F32R)
        raw = sb("raw", [P, 2, BT, LC, DC])
        rot = sb("rot", [P, BT, LC, DC])
        half = sb("half", [P, BT, LC, DC])
        kv_hi, kv_lo = sb("kv_hi", [P, 2, BT, LC, DC], F32R), sb("kv_lo", [P, 2, BT, LC, DC], F32R)
        kT_hi, kT_lo = sb("kT_hi", [P, 2, BT, LP], F32R), sb("kT_lo", [P, 2, BT, LP], F32R)
        last = sb("last", [1, GB, DC])
        attn = sb("attn", [P, 3, 4, L])
        aT_hi, aT_lo = sb("aT_hi", [P, LC, BANK], F32R), sb("aT_lo", [P, LC, BANK], F32R)
        aT_last = sb("aT_last", [1, BANK])
        negmax, total, recip = (sb(n, [P, 3, 4]) for n in ("negmax", "total", "recip"))
        out = sb("out", [P, H, P])
        zero = sb("zero", [P, D])

        NB = 4
        ring = [ctx.enter_context(nc.psum_tensor(f"x_ring{n}", [P, BANK], F32)) for n in range(NB)]
        score = [ctx.enter_context(nc.psum_tensor(f"x_score{n}", [P, BANK], F32)) for n in range(4)]

        table_in, raw_in, last_in = sem("table_in"), [sem("raw_in0"), sem("raw_in1")], sem("last_in")
        rot_done, nat_hi, kv_done, raw_free = sem("rot_done"), sem("nat_hi"), sem("kv_done"), sem("raw_free")
        ready, hi_done, free = sem("ready"), sem("hi"), sem("free")
        score_ready, max_done, exp_done = sem("score_ready"), sem("max_done"), sem("exp_done")
        recip_done, norm_done = sem("recip_done"), sem("norm_done")
        out_done, pad_done, zero_done, zero_out = sem("out_done"), sem("pad_done"), sem("zero_done"), sem("zero_out")

        AHEAD, LAG = 2, 2
        steps = []
        for j in range(PAIRS):
            steps += [("qp", j)] + ([("qr", j + AHEAD)] if j + AHEAD < PAIRS else [])
            if j in (1, 6):
                steps += [("kT", j // 5, c) for c in range(LC)]
        for b in range(GB + LAG):
            if b >= LAG:
                steps += [("aT", b - LAG, c) for c in (LC, *range(LC))]
            if b < GB:
                steps += [("sc", b)]
            elif b == GB + LAG - 1:
                steps += [("qr", 0), ("qr", 1)]
            if b >= LAG:
                steps += [("av", b - LAG)]
            if b < GB:
                steps += [("rc", b)]
        kinds = ("qr", "qp", "kT", "aT", "av")
        splits = ("qr", "qp", "kT")
        job = {s: n + AHEAD + 1 for n, s in enumerate([s for s in steps if s[0] in kinds])}
        split = {s: n + AHEAD for n, s in enumerate([s for s in job if s[0] in splits or (s[0] == "aT" and s[2] < LC)])}
        NJ, NS = len(job), len(split)

        def tokens_of(s, i):
            return (i + 1) & (SG - 1) if s[1] < AHEAD else i

        def qr_ready(j):
            return job["qr", j] - NJ if j < AHEAD else job["qr", j]

        assert NJ % NB == 0

        with nc.Block() as block:
            @block.sync
            def _(sp):
                sp.dma_start(cos[:, :, :], A["cos"]).then_inc(table_in, 16)
                sp.dma_start(sin[:, :, :], A["sin"]).then_inc(table_in, 16)
                kv_d = A["ctx"][:, 0:LC * P, :].rearrange("(g b) (c p) d -> g p b c d", b=BT, p=P)
                last_d = sh.last_dram.rearrange("(i o b) d -> i o b d", o=1, b=GB)
                def load_keys(i, k):
                    sp.wait_ge(raw_free, 3 * (2 * i + k + 1))
                    for b in range(BT):
                        sp.dma_start(raw[:, k, b], kv_d[2 * i + k, :, b]).then_inc(raw_in[k], 16)

                def store_tile(i, k):
                    sp.wait_ge(free, NB + NJ * i + job["av", 4 * k + 3] + 1)
                    sp.dma_start(sh.ctx_dram[2 * i + k], out[:, :, :].rearrange("p h t -> p (h t)")).then_inc(out_done, 16)

                def last_row(i):
                    sp.dma_start(last[:, :, :], last_d[i]).then_inc(last_in, 16)

                unfilled = sh.sorted_dram.rearrange("(i n p) d -> i p n d", i=SG, p=P)
                unused = sh.y_dram[E * CAP:].rearrange("(i n p) d -> i p n d", i=SG, p=P)
                sp.wait_ge(zero_done, 1)

                def fill(i):
                    for rows in (unfilled, unused):
                        sp.dma_start(rows[i], zero[:, :].unsqueeze(1).to_broadcast([P, rows.shape[2], D])).then_inc(zero_out, 16)

                load_keys(0, 0)
                load_keys(0, 1)
                last_row(0)
                with sp.Fori(0, SG - 1) as i:
                    load_keys(i + 1, 0)
                    load_keys(i + 1, 1)
                    fill(i)
                    store_tile(i, 0)
                    store_tile(i, 1)
                    last_row(i + 1)
                fill(SG - 1)
                store_tile(SG - 1, 0)
                store_tile(SG - 1, 1)
                sp.wait_ge(zero_out, 16 * 2 * SG)
                sp.wait_ge(out_done, 16 * (2 * SG + 1))

            @block.gpsimd
            def _(pool):
                nc.gpsimd.memset(zero[:, :], 0.0).then_inc(zero_done, 1)
                nc.gpsimd.memset(kT_hi[:, :, :, L:LP].bitcast(F32), 0.0).then_inc(pad_done, 1)
                nc.gpsimd.memset(kT_lo[:, :, :, L:LP].bitcast(F32), 0.0).then_inc(pad_done, 1)
                pool.sem_inc(raw_free, 6)
                pool.wait_ge(table_in, 32)
                with pool.Fori(0, SG) as i:
                    for k in range(2):
                        pool.wait_ge(raw_in[k], 16 * BT * (i + 1))
                        if k == 1:
                            pool.wait_ge(ready, NJ * i + job["kT", 0, LC - 1] + 1)
                        v, o = raw[:, k].rearrange("p b c d -> p b (c d)"), rot[:, :].rearrange("p b c d -> p b (c d)")
                        cb = cos[:, :, :].rearrange("p c d -> p (c d)").unsqueeze(1).to_broadcast([P, BT, LC * DC])
                        nc.gpsimd.tensor_tensor(o, v, cb, ALU.mult).then_inc(raw_free, 1)
                        for a in range(2):
                            to, of = slice(64 * a, 64 * a + 64), slice(64 - 64 * a, 128 - 64 * a)
                            sb_ = sin[:, :, to].unsqueeze(1).to_broadcast([P, BT, LC, 64])
                            nc.gpsimd.tensor_tensor(half[:, :, :, to], raw[:, k, :, :, of], sb_, ALU.mult).then_inc(raw_free, 1)
                        pool.wait_ge(raw_free, 6 + 3 * (2 * i + k + 1))
                        nc.gpsimd.tensor_tensor(o, o, half[:, :].rearrange("p b c d -> p b (c d)"), ALU.add).then_inc(rot_done, 1)
                        pool.wait_ge(rot_done, 2 * i + k + 1)
                        pool.wait_ge(nat_hi, 2 * i + k + 1)
                        for kT, lT in ((kT_hi, sh.lastT_hi), (kT_lo, sh.lastT_lo)):
                            nc.gpsimd.tensor_copy(kT[:, k, :, L - 1:L],
                                                  lT[:, bass.ds(i * GB + k * BT, BT)].bitcast(F32).unsqueeze(2)).then_inc(kv_done, 1)
                        nc.gpsimd.tensor_tensor(kv_lo[:, k], rot[:, :], kv_hi[:, k].bitcast(F32), ALU.subtract).then_inc(kv_done, 1)
                        pool.wait_ge(kv_done, 3 * (2 * i + k + 1))
                    for b in range(GB):
                        pool.wait_ge(recip_done, GB * i + b + 1)
                        nc.gpsimd.tensor_tensor(attn[:, b % 3], attn[:, b % 3], recip[:, b % 3].unsqueeze(2).to_broadcast([P, 4, L]),
                                                ALU.mult).then_inc(norm_done, 1)

            @block.scalar
            def _(act):
                for j in range(AHEAD):
                    act.wait_ge(ready, j + 1)
                    nc.scalar.copy(qr_hi[:, j % NQ], ring[j][:, 0:GT]).then_inc(hi_done, 1)
                with act.Fori(0, SG) as i:
                    def hi_copy(s, dst, src):
                        act.wait_ge(ready, NJ * i + job[s] + 1)
                        nc.scalar.copy(dst, src).then_inc(hi_done, 1)

                    for s in steps:
                        bank = ring[job[s] % NB] if s in job else None
                        if s[0] == "qr":
                            hi_copy(s, qr_hi[:, s[1] % NQ], bank[:, 0:GT])
                        elif s[0] == "qp":
                            j = s[1]
                            hi_copy(s, qp_hi[:, :, 2 * j:2 * j + 2, :].rearrange("p b h s -> p h b s"),
                                    bank[:, :].rearrange("p (h b s) -> p h b s", h=2, b=GB))
                        elif s[0] == "kT":
                            _, k, c = s
                            hi_copy(s, kT_hi[:, k, :, c * P:(c + 1) * P], bank[:, :].rearrange("p (b l) -> p b l", b=BT))
                            if c == LC - 1:
                                act.wait_ge(rot_done, 2 * i + k + 1)
                                nc.scalar.copy(kv_hi[:, k], rot[:, :]).then_inc(nat_hi, 1)
                        elif s[0] == "aT" and s[2] < LC:
                            hi_copy(s, aT_hi[:, s[2]], bank[:, :])
                        elif s[0] == "sc":
                            b = s[1]
                            for g in range(4):
                                act.wait_ge(max_done, 4 * GB * i + 4 * b + g + 1)
                                nc.scalar.activation(attn[:, b % 3, g], score[g][:, 0:L], ACT.Exp, bias=negmax[:, b % 3, g:g + 1],
                                                     accum_out=total[:, b % 3, g:g + 1]).then_inc(exp_done, 1)

            @block.vector
            def _(dve):
                dve.sem_inc(free, NB)
                dve.sem_inc(out_done, 16)
                for j in range(AHEAD):
                    dve.wait_ge(hi_done, j + 1)
                    split_lo(nc, qr_lo[:, j % NQ], ring[j][:, 0:GT], qr_hi[:, j % NQ]).then_inc(free, 1)
                dve.wait_ge(free, NB + AHEAD)
                dve.sem_inc(free, 1)
                with dve.Fori(0, SG) as i:
                    for s in steps:
                        bank = ring[job[s] % NB] if s in job else None
                        if s in split:
                            dve.wait_ge(hi_done, NS * i + split[s] + 1)
                        elif s in job:
                            dve.wait_ge(ready, NJ * i + job[s] + 1)
                        if s[0] == "qr":
                            split_lo(nc, qr_lo[:, s[1] % NQ], bank[:, 0:GT], qr_hi[:, s[1] % NQ]).then_inc(free, 1)
                        elif s[0] == "qp":
                            at = slice(2 * s[1], 2 * s[1] + 2)
                            split_lo(nc, qp_lo[:, :, at, :].rearrange("p b h s -> p h b s"),
                                     bank[:, :].rearrange("p (h b s) -> p h b s", h=2, b=GB),
                                     qp_hi[:, :, at, :].rearrange("p b h s -> p h b s")).then_inc(free, 1)
                        elif s[0] == "kT":
                            _, k, c = s
                            at = slice(c * P, (c + 1) * P)
                            split_lo(nc, kT_lo[:, k, :, at], bank[:, :].rearrange("p (b l) -> p b l", b=BT), kT_hi[:, k, :, at]).then_inc(free, 1)
                        elif s[0] == "sc":
                            b = s[1]
                            for g in range(4):
                                dve.wait_ge(score_ready, 4 * GB * i + 4 * b + g + 1)
                                nc.vector.tensor_reduce(negmax[:, b % 3, g:g + 1], score[g][:, 0:L], AX, ALU.max, negate=True).then_inc(max_done, 1)
                        elif s[0] == "rc":
                            b = s[1]
                            dve.wait_ge(exp_done, 4 * GB * i + 4 * b + 4)
                            nc.vector.reciprocal(recip[:, b % 3], total[:, b % 3]).then_inc(recip_done, 1)
                        elif s[0] == "aT":
                            c = s[2]
                            if c < LC:
                                split_lo(nc, aT_lo[:, c], bank[:, :], aT_hi[:, c]).then_inc(free, 1)
                            else:
                                nc.vector.tensor_copy(aT_last[:, :], bank[0:1, :]).then_inc(free, 1)
                        elif s[0] == "av":
                            b = s[1]
                            if b % BT == 0:
                                dve.wait_ge(out_done, 16 * (2 * i + b // BT + 1))
                            nc.vector.tensor_copy(out[:, :, (b % BT) * S:(b % BT + 1) * S],
                                                  bank[:, :].rearrange("p (h s) -> p h s", h=H)).then_inc(free, 1)

            @block.tensor
            def _(pe):
                pe.wait_ge(pad_done, 2)

                def score_rank(bank, j, group):
                    w, at = slice(j * P, (j + 1) * P), bass.ds(group * GT, GT)
                    for c in range(DCH):
                        mm = three_passes(nc, bank[:, 0:GT], sh.m1_hi[:, c, w], sh.m1_lo[:, c, w],
                                          sh.xT_hi[:, c, at], sh.xT_lo[:, c, at], c == 0, c == DCH - 1)
                    mm.then_inc(ready, 1)

                for j in range(AHEAD):
                    pe.wait_ge(free, j + 1)
                    score_rank(ring[j], j, 0)
                pe.wait_ge(ready, AHEAD)
                pe.sem_inc(ready, 1)
                with pe.Fori(0, SG) as i:
                    for s in steps:
                        n = job.get(s)
                        if n is not None:
                            bank = ring[n % NB]
                            pe.wait_ge(free, NJ * i + n + 1)
                        if s[0] == "qr":
                            score_rank(bank, s[1], tokens_of(s, i))
                        elif s[0] == "qp":
                            j = s[1]
                            pe.wait_ge(free, NB + NJ * i + qr_ready(j) + 1)
                            for e in range(2):
                                mm = three_passes(nc, bank[:, e * GT:(e + 1) * GT], sh.krT_hi[:, 2 * j + e], sh.krT_lo[:, 2 * j + e],
                                                  qr_hi[:, j % NQ], qr_lo[:, j % NQ], True, True)
                            mm.then_inc(ready, 1)
                        elif s[0] == "kT":
                            _, k, c = s
                            pe.wait_ge(rot_done, 2 * i + k + 1)
                            for b in range(BT):
                                mm = nc.tensor.transpose(bank[:, b * P:(b + 1) * P], rot[:, b, c], sh.ident[:, :])
                            mm.then_inc(ready, 1)
                        elif s[0] == "sc":
                            b = s[1]
                            k = b // BT
                            if b % BT == 0:
                                pe.wait_ge(kv_done, 3 * (2 * i + k + 1))
                                pe.wait_ge(free, NB + NJ * i + (job["qp", PAIRS - 1] if k == 0 else job["kT", 1, LC - 1]) + 1)
                            for g in range(4):
                                lhs = [q[:, b, 4 * g:4 * g + 4, :].rearrange("p h s -> p (h s)") for q in (qp_hi, qp_lo)]
                                if b > 0:
                                    pe.wait_ge(exp_done, 4 * GB * i + 4 * (b - 1) + g + 1)
                                three_passes(nc, score[g][:, 0:LP], lhs[0], lhs[1], kT_hi[:, k, b % BT], kT_lo[:, k, b % BT],
                                             True, True).then_inc(score_ready, 1)
                        elif s[0] == "aT":
                            _, b, c = s
                            if c == LC:
                                pe.wait_ge(norm_done, GB * i + b + 1)
                            w = P if c < LC else 1
                            for g in range(4):
                                mm = nc.tensor.transpose(bank[0:w, g * P:(g + 1) * P], attn[:, b % 3, g, c * P:c * P + w], sh.ident[:, :])
                            mm.then_inc(ready, 1)
                        elif s[0] == "av":
                            b = s[1]
                            k = b // BT
                            if b == 0:
                                pe.wait_ge(last_in, 16 * (i + 1))
                            pe.wait_ge(free, NB + NJ * i + job["aT", b, LC] + 1)
                            nc.tensor.matmul(bank[:, :], last[0:1, b, :], aT_last[:, :], start=True, stop=False)
                            for c in range(LC):
                                pe.wait_ge(free, NB + NJ * i + job["aT", b, c] + 1)
                                mm = three_passes(nc, bank[:, :], kv_hi[:, k, b % BT, c], kv_lo[:, k, b % BT, c],
                                                  aT_hi[:, c], aT_lo[:, c], False, c == LC - 1)
                            mm.then_inc(ready, 1)


def project_context(nc, A, sh):
    with ExitStack() as ctx:
        def sb(name, shape, dt=F32):
            return ctx.enter_context(nc.sbuf_tensor("o_" + name, shape, dt))

        def sem(name):
            return ctx.enter_context(nc.semaphore("o_" + name))

        HG, NW = 4, 3
        wo = sb("wo", [P, DCH, H * P])
        kckv = sb("kckv", [P, H, DC])
        woT = sb("woT", [P, NW, D])
        wm_hi, wm_lo = sb("wm_hi", [P, H, D], F32R), sb("wm_lo", [P, H, D], F32R)
        raw = sb("raw", [P, 2, H, P])
        c_hi, c_lo = sb("c_hi", [P, 2, H, P], F32R), sb("c_lo", [P, 2, H, P], F32R)
        NB = 6
        ring = [ctx.enter_context(nc.psum_tensor(f"o_ring{n}", [P, BANK], F32)) for n in range(NB)]
        acc = [ctx.enter_context(nc.psum_tensor(f"o_acc{n}", [P, BANK], F32)) for n in range(2)]

        wo_in, kckv_in, x_in = [sem(f"wo_in{g}") for g in range(H // HG)], sem("kckv_in"), sem("x_in")
        raw_in = [sem("raw_in0"), sem("raw_in1")]
        ready, hi_done, free = sem("ready"), sem("hi"), sem("free")
        c_hi_done, c_lo_done, acc_ready, acc_free = sem("c_hi_done"), sem("c_lo_done"), sem("acc_ready"), sem("acc_free")

        steps = [("woT", 0), ("woT", 1)]
        for h in range(H):
            steps += ([("woT", h + 2)] if h + 2 < H else []) + [("wm", h)]
        job = {s: n for n, s in enumerate(steps)}
        split = numbered(steps, ("wm",))

        with nc.Block() as block:
            @block.sync
            def _(sp):
                wo_d = A["Wo"].rearrange("(c o) n -> o c n", o=P)
                for g in range(H // HG):
                    at = slice(g * HG * P, (g + 1) * HG * P)
                    sp.dma_start(wo[:, :, at], wo_d[:, :, at]).then_inc(wo_in[g], 16)
                    if g == 0:
                        sp.dma_start(kckv[:, :, :], A["w_kc_kv"].rearrange("h k c -> k h c")).then_inc(kckv_in, 16)
                sp.dma_start(sh.x[:, :, :], A["x"].rearrange("b s d -> (b s) d").rearrange("(n p) d -> p n d", p=P)).then_inc(x_in, 16)
                with sp.Fori(0, NT // 2) as i:
                    for k in range(2):
                        sp.wait_ge(c_lo_done, 2 * i + k + 1)
                        sp.dma_start(raw[:, k].rearrange("p h t -> p (h t)"), sh.ctx_dram[2 * i + k]).then_inc(raw_in[k], 16)

            @block.scalar
            def _(act):
                for s in steps:
                    if s[0] == "wm":
                        act.wait_ge(ready, job[s] + 1)
                        nc.scalar.copy(wm_hi[:, s[1]], ring[job[s] % NB][:, :]).then_inc(hi_done, 1)
                with act.Fori(0, NT // 2) as i:
                    for k in range(2):
                        act.wait_ge(raw_in[k], 16 * (i + 1))
                        act.wait_ge(acc_ready, 2 * i + k + 1)
                        nc.scalar.copy(c_hi[:, k], raw[:, k]).then_inc(c_hi_done, 1)

            @block.vector
            def _(dve):
                dve.sem_inc(c_lo_done, 2)
                dve.sem_inc(acc_free, 2)
                for s in steps:
                    bank = ring[job[s] % NB]
                    if s[0] == "wm":
                        dve.wait_ge(hi_done, split[s] + 1)
                        split_lo(nc, wm_lo[:, s[1]], bank[:, :], wm_hi[:, s[1]]).then_inc(free, 1)
                    else:
                        dve.wait_ge(ready, job[s] + 1)
                        nc.vector.tensor_copy(woT[:, s[1] % NW], bank[:, :]).then_inc(free, 1)
                dve.wait_ge(x_in, 16)

                def c_split(k, hi_count):
                    dve.wait_ge(c_hi_done, hi_count)
                    nc.vector.tensor_tensor(c_lo[:, k], raw[:, k], c_hi[:, k].bitcast(F32), ALU.subtract).then_inc(c_lo_done, 1)

                c_split(0, 1)
                with dve.Fori(0, NT // 2 - 1) as i:
                    for k in range(2):
                        c_split(1 - k, 2 * i + k + 2)
                        dve.wait_ge(acc_ready, 2 + 2 * i + k + 1)
                        at = sh.x[:, bass.ds(2 * i + k, 1), :].rearrange("p n d -> p (n d)")
                        nc.vector.tensor_tensor(at, acc[k][:, :], at, ALU.add).then_inc(acc_free, 1)
                c_split(1, NT)
                for k in range(2):
                    dve.wait_ge(acc_ready, 2 + NT - 2 + k + 1)
                    nc.vector.tensor_tensor(sh.x[:, NT - 2 + k], acc[k][:, :], sh.x[:, NT - 2 + k], ALU.add).then_inc(acc_free, 1)

            @block.tensor
            def _(pe):
                pe.sem_inc(acc_ready, 2)
                for s in steps:
                    n, h = job[s], s[1]
                    bank = ring[n % NB]
                    if n >= NB:
                        pe.wait_ge(free, n - NB + 1)
                    if s[0] == "woT":
                        if h % HG == 0:
                            pe.wait_ge(wo_in[h // HG], 16)
                        for c in range(DCH):
                            mm = nc.tensor.transpose(bank[:, c * P:(c + 1) * P], wo[:, c, h * P:(h + 1) * P], sh.ident[:, :])
                    else:
                        pe.wait_ge(kckv_in, 16)
                        pe.wait_ge(free, job["woT", h] + 1)
                        mm = nc.tensor.matmul(bank[:, :], kckv[:, h], woT[:, h % NW], start=True, stop=True)
                    mm.then_inc(ready, 1)
                pe.wait_ge(free, len(steps))
                with pe.Fori(0, NT // 2) as i:
                    for k in range(2):
                        pe.wait_ge(c_lo_done, 2 + 2 * i + k + 1)
                        pe.wait_ge(acc_free, 2 * i + k + 1)
                        for h in range(H):
                            mm = three_passes(nc, acc[k][:, :], c_hi[:, k, h], c_lo[:, k, h], wm_hi[:, h], wm_lo[:, h], h == 0, h == H - 1)
                        mm.then_inc(acc_ready, 1)


def self_attention(nc, A, sh):
    with ExitStack() as ctx:
        def sb(name, shape, dt=F32):
            return ctx.enter_context(nc.sbuf_tensor("s_" + name, shape, dt))

        def sem(name):
            return ctx.enter_context(nc.semaphore("s_" + name))

        SCALE = float(1.0 / np.sqrt(P))
        HALVES = T // BANK
        BH = B // HALVES
        xn = sb("xn", [P, 2, D])
        xT_hi, xT_lo = sb("xT_hi", [P, DCH, T], F32R), sb("xT_lo", [P, DCH, T], F32R)
        wq, wk, wo = sb("wq", [P, G, D]), sb("wk", [P, D]), sb("wo", [P, DCH, G * P])
        wqT_hi, wqT_lo = sb("wqT_hi", [P, DCH, G * P], F32R), sb("wqT_lo", [P, DCH, G * P], F32R)
        wkT_hi, wkT_lo = sb("wkT_hi", [P, DCH, P], F32R), sb("wkT_lo", [P, DCH, P], F32R)
        woT_hi, woT_lo = sb("woT_hi", [P, G, D], F32R), sb("woT_lo", [P, G, D], F32R)
        kT = sb("kT", [P, T])
        qT = sb("qT", [P, B, G, S])
        v_all = sb("v_all", [P, NT, KVH * P])
        v = sb("v", [P, NT, P])
        mask = sb("mask", [P, S])
        prob = sb("prob", [P, HALVES, BH, S])
        peak, total, recip = (sb(n, [P, HALVES, BH]) for n in ("peak", "total", "recip"))
        pT = sb("pT", [P, HALVES, BANK])
        o_hi, o_lo = sb("o_hi", [P, G, T], F32R), sb("o_lo", [P, G, T], F32R)
        wv = qT[:, :, :, :].rearrange("p b g s -> p (b g s)")[:, 0:KVH * D].rearrange("p (c d) -> p c d", c=KVH)
        wvT_hi = o_hi[:, 0:2, :].rearrange("p g t -> p (g t)").rearrange("p (c n) -> p c n", c=DCH)
        wvT_lo = o_lo[:, 0:2, :].rearrange("p g t -> p (g t)").rearrange("p (c n) -> p c n", c=DCH)
        ln = LayerNorm(nc, ctx, "s_ln")
        NB, NA = 4, 2
        ring = [ctx.enter_context(nc.psum_tensor(f"s_ring{n}", [P, BANK], F32)) for n in range(NB)]
        score = [ctx.enter_context(nc.psum_tensor(f"s_score{n}", [P, BANK], F32)) for n in range(HALVES)]

        wq_in, wk_in, wo_in, wv_in, mask_in = (sem(n) for n in ("wq_in", "wk_in", "wo_in", "wv_in", "mask_in"))
        xn_done, v_done = sem("xn_done"), sem("v_done")
        pready, phi, pfree = sem("pready"), sem("phi"), sem("pfree")
        ready, hi_done, free = sem("ready"), sem("hi"), sem("free")
        score_ready, prob_done, shifted, exp_done, soft = (sem(n) for n in ("score_ready", "prob_done", "shifted", "exp_done", "soft"))

        first = [("wvT", c) for c in range(DCH)] + [("xT", t) for t in range(NT)] + [("v", t) for t in range(NT)]
        fjob, fsplit = {s: n for n, s in enumerate(first)}, numbered(first, ("wvT", "xT"))

        steps = [("wkT", c) for c in range(DCH)] + [("wqT", c) for c in range(DCH)] + [("kT", a) for a in range(HALVES)]
        steps += [("qT", g, 0) for g in range(G)] + [("sc", 0)]
        steps += [("woT", g) for g in range(G)]
        steps += [("qT", g, 1) for g in range(G)] + [("sc", 1), ("pT", 0)]
        steps += [("oT", 0, b) for b in range(BT)] + [("out", t) for t in range(NT // 2)] + [("pT", 1)]
        steps += [("oT", 1, b) for b in range(BT)] + [("out", t) for t in range(NT // 2, NT)]
        job = numbered(steps, ("wkT", "wqT", "woT", "kT", "qT", "pT", "oT", "out"))
        split = numbered(steps, ("wkT", "wqT", "woT", "oT"))
        NJ, NS = len(job), len(split)
        assert NJ % NB == 0
        SOFT = 5

        def o_at(o, a, b):
            return o[:, :, a * BANK:(a + 1) * BANK].rearrange("p g (n b t) -> p n b g t", n=BH // BT, b=BT)[:, :, b]

        with nc.Block() as block:
            @block.sync
            def _(sp):
                sp.dma_start(wv, A["wv"].rearrange("(c k) d -> k c d", k=P)).then_inc(wv_in, 16)
                sp.dma_start(mask[:, :], A["mask"]).then_inc(mask_in, 16)
                wq_d = A["wq"].rearrange("(j g k) d -> j k g d", g=G, k=P)
                wk_d = A["wk"].rearrange("(j k) d -> j k d", k=P)
                wo_d = A["wo"].rearrange("(c o) (j n) -> j o c n", o=P, j=KVH)
                with sp.Fori(0, KVH) as i:
                    sp.wait_ge(ready, NJ * i + job["wqT", DCH - 1] + 1)
                    sp.dma_start(wk[:, :], wk_d[i]).then_inc(wk_in, 16)
                    sp.dma_start(wq[:, :, :], wq_d[i]).then_inc(wq_in, 16)
                    sp.wait_ge(ready, NJ * i + job["woT", G - 1] + 1)
                    sp.dma_start(wo[:, :, :], wo_d[i]).then_inc(wo_in, 16)

            @block.gpsimd
            def _(pool):
                with pool.Fori(0, KVH) as i:
                    pool.wait_ge(pfree, len(first) + NB)
                    pool.wait_ge(ready, NJ + NJ * i + job["wkT", 0] + 1)
                    nc.gpsimd.tensor_copy(v[:, :, :], v_all[:, :, bass.ds(i * P, P)]).then_inc(v_done, 1)

            @block.scalar
            def _(act):
                ln.take_root(act, 0, NT)
                for s in first:
                    bank = ring[fjob[s] % NB]
                    if s in fsplit:
                        act.wait_ge(pready, fjob[s] + 1)
                        if s[0] == "wvT":
                            nc.scalar.copy(wvT_hi[:, s[1]], bank[:, :]).then_inc(phi, 1)
                        else:
                            nc.scalar.copy(xT_hi[:, :, s[1] * P:(s[1] + 1) * P], bank[:, :].rearrange("p (c t) -> p c t", c=DCH)).then_inc(phi, 1)
                with act.Fori(0, KVH) as i:
                    for s in steps:
                        if s in split:
                            bank = ring[job[s] % NB]
                            act.wait_ge(ready, NJ + NJ * i + job[s] + 1)
                        if s[0] == "wkT":
                            nc.scalar.copy(wkT_hi[:, s[1]], bank[:, 0:P]).then_inc(hi_done, 1)
                        elif s[0] == "wqT":
                            nc.scalar.copy(wqT_hi[:, s[1]], bank[:, :]).then_inc(hi_done, 1)
                        elif s[0] == "woT":
                            nc.scalar.copy(woT_hi[:, s[1]], bank[:, :]).then_inc(hi_done, 1)
                        elif s[0] == "oT":
                            nc.scalar.copy(o_at(o_hi, s[1], s[2]), bank[:, :].rearrange("p (n g t) -> p n g t", n=BH // BT, g=G)).then_inc(hi_done, 1)
                        elif s[0] == "sc":
                            a = s[1]
                            act.wait_ge(shifted, HALVES * i + a + 1)
                            nc.scalar.activation(prob[:, a], prob[:, a], ACT.Exp).then_inc(exp_done, 1)

            @block.vector
            def _(dve):
                for t in range(NT):
                    ln.statistics(dve, sh.x[:, t], t)
                ln.variance(dve, 0, NT)
                ln.power(dve, 0, NT)

                def norm(t):
                    if t >= 2:
                        dve.wait_ge(pready, fjob["xT", t - 2] + 1)
                    ln.apply(t, xn[:, t % 2], sh.x[:, t]).then_inc(xn_done, 1)

                norm(0)
                norm(1)
                dve.sem_inc(pfree, NB)
                for s in first:
                    bank = ring[fjob[s] % NB]
                    if s in fsplit:
                        dve.wait_ge(phi, fsplit[s] + 1)
                    else:
                        dve.wait_ge(pready, fjob[s] + 1)
                    if s[0] == "wvT":
                        split_lo(nc, wvT_lo[:, s[1]], bank[:, :], wvT_hi[:, s[1]]).then_inc(pfree, 1)
                    elif s[0] == "xT":
                        at = slice(s[1] * P, (s[1] + 1) * P)
                        split_lo(nc, xT_lo[:, :, at], bank[:, :].rearrange("p (c t) -> p c t", c=DCH), xT_hi[:, :, at]).then_inc(pfree, 1)
                        if s[1] + 2 < NT:
                            norm(s[1] + 2)
                    else:
                        nc.vector.tensor_copy(v_all[:, s[1]], bank[:, :]).then_inc(pfree, 1)
                dve.wait_ge(mask_in, 16)
                dve.sem_inc(free, NB)
                with dve.Fori(0, KVH) as i:
                    def chained(instruction, a, n):
                        instruction.then_inc(soft, 1)
                        dve.wait_ge(soft, SOFT * (HALVES * i + a) + n)

                    for s in steps:
                        bank = ring[job[s] % NB] if s in job else None
                        if s in split:
                            dve.wait_ge(hi_done, NS * i + split[s] + 1)
                        elif s in job:
                            dve.wait_ge(ready, NJ + NJ * i + job[s] + 1)
                        if s[0] == "wkT":
                            split_lo(nc, wkT_lo[:, s[1]], bank[:, 0:P], wkT_hi[:, s[1]]).then_inc(free, 1)
                        elif s[0] == "wqT":
                            split_lo(nc, wqT_lo[:, s[1]], bank[:, :], wqT_hi[:, s[1]]).then_inc(free, 1)
                        elif s[0] == "woT":
                            split_lo(nc, woT_lo[:, s[1]], bank[:, :], woT_hi[:, s[1]]).then_inc(free, 1)
                        elif s[0] == "kT":
                            nc.vector.tensor_copy(kT[:, s[1] * BANK:(s[1] + 1) * BANK], bank[:, :]).then_inc(free, 1)
                        elif s[0] == "qT":
                            _, g, a = s
                            nc.vector.tensor_copy(qT[:, a * BH:(a + 1) * BH, g, :], bank[:, :].rearrange("p (b t) -> p b t", b=BH)).then_inc(free, 1)
                        elif s[0] == "sc":
                            a = s[1]
                            dve.wait_ge(score_ready, HALVES * i + a + 1)
                            chained(nc.vector.scalar_tensor_tensor(
                                prob[:, a], score[a][:, :].rearrange("p (b s) -> p b s", b=BH), SCALE,
                                mask[:, :].unsqueeze(1).to_broadcast([P, BH, S]), ALU.mult, ALU.add), a, 1)
                            chained(nc.vector.tensor_reduce(peak[:, a], prob[:, a], AX, ALU.max), a, 2)
                            nc.vector.tensor_tensor(prob[:, a], prob[:, a], peak[:, a].unsqueeze(2).to_broadcast([P, BH, S]),
                                                    ALU.subtract).then_inc(shifted, 1)
                        elif s[0] == "pT":
                            nc.vector.tensor_copy(pT[:, s[1]], bank[:, :]).then_inc(free, 1)
                        elif s[0] == "oT":
                            split_lo(nc, o_at(o_lo, s[1], s[2]), bank[:, :].rearrange("p (n g t) -> p n g t", n=BH // BT, g=G),
                                     o_at(o_hi, s[1], s[2])).then_inc(free, 1)
                        elif s[0] == "out":
                            nc.vector.tensor_tensor(sh.x[:, s[1]], bank[:, :], sh.x[:, s[1]], ALU.add).then_inc(free, 1)
                        if s in (("woT", G - 1), ("sc", 1)):
                            a = 0 if s[0] == "woT" else 1
                            dve.wait_ge(exp_done, HALVES * i + a + 1)
                            chained(nc.vector.tensor_reduce(total[:, a], prob[:, a], AX, ALU.add), a, 3)
                            chained(nc.vector.tensor_scalar_max(total[:, a], total[:, a], 1e-9), a, 4)
                            chained(nc.vector.reciprocal(recip[:, a], total[:, a]), a, 5)
                            nc.vector.tensor_tensor(prob[:, a], prob[:, a], recip[:, a].unsqueeze(2).to_broadcast([P, BH, S]),
                                                    ALU.mult).then_inc(prob_done, 1)

            @block.tensor
            def _(pe):
                pe.sem_inc(ready, NJ)
                for s in first:
                    n = fjob[s]
                    bank = ring[n % NB]
                    pe.wait_ge(pfree, n + 1)
                    if s[0] == "wvT":
                        pe.wait_ge(wv_in, 16)
                        for j in range(KVH):
                            mm = nc.tensor.transpose(bank[:, j * P:(j + 1) * P], wv[:, j, s[1] * P:(s[1] + 1) * P], sh.ident[:, :])
                    elif s[0] == "xT":
                        pe.wait_ge(xn_done, s[1] + 1)
                        for c in range(DCH):
                            mm = nc.tensor.transpose(bank[:, c * P:(c + 1) * P], xn[:, s[1] % 2, c * P:(c + 1) * P], sh.ident[:, :])
                    else:
                        pe.wait_ge(pfree, NB + fjob["xT", NT - 1] + 1)
                        at = slice(s[1] * P, (s[1] + 1) * P)
                        for c in range(DCH):
                            mm = three_passes(nc, bank[:, :], xT_hi[:, c, at], xT_lo[:, c, at], wvT_hi[:, c], wvT_lo[:, c], c == 0, c == DCH - 1)
                    mm.then_inc(pready, 1)
                pe.wait_ge(pfree, NB + len(first))
                with pe.Fori(0, KVH) as i:
                    def settled(s):
                        pe.wait_ge(free, NB + NJ * i + job[s] + 1)

                    for s in steps:
                        if s in job:
                            bank = ring[job[s] % NB]
                            pe.wait_ge(free, NJ * i + job[s] + 1)
                        if s[0] == "wkT":
                            if s[1] == 0:
                                pe.wait_ge(wk_in, 16 * (i + 1))
                            mm = nc.tensor.transpose(bank[:, 0:P], wk[:, s[1] * P:(s[1] + 1) * P], sh.ident[:, :])
                        elif s[0] == "wqT":
                            if s[1] == 0:
                                pe.wait_ge(wq_in, 16 * (i + 1))
                            for g in range(G):
                                mm = nc.tensor.transpose(bank[:, g * P:(g + 1) * P], wq[:, g, s[1] * P:(s[1] + 1) * P], sh.ident[:, :])
                        elif s[0] == "woT":
                            if s[1] == 0:
                                pe.wait_ge(wo_in, 16 * (i + 1))
                            for c in range(DCH):
                                mm = nc.tensor.transpose(bank[:, c * P:(c + 1) * P], wo[:, c, s[1] * P:(s[1] + 1) * P], sh.ident[:, :])
                        elif s[0] == "kT":
                            settled(("wkT", DCH - 1))
                            at = slice(s[1] * BANK, (s[1] + 1) * BANK)
                            for c in range(DCH):
                                mm = three_passes(nc, bank[:, :], wkT_hi[:, c], wkT_lo[:, c], xT_hi[:, c, at], xT_lo[:, c, at], c == 0, c == DCH - 1)
                        elif s[0] == "qT":
                            _, g, a = s
                            settled(("wqT", DCH - 1))
                            at, w = slice(a * BANK, (a + 1) * BANK), slice(g * P, (g + 1) * P)
                            for c in range(DCH):
                                mm = three_passes(nc, bank[:, :], wqT_hi[:, c, w], wqT_lo[:, c, w], xT_hi[:, c, at], xT_lo[:, c, at], c == 0, c == DCH - 1)
                        elif s[0] == "sc":
                            a = s[1]
                            settled(("qT", G - 1, a))
                            for n in range(BH):
                                b = a * BH + n
                                mm = nc.tensor.matmul(score[a][:, n * S:(n + 1) * S], qT[:, b].rearrange("p g s -> p (g s)"), kT[:, b * S:(b + 1) * S],
                                                      start=True, stop=True)
                            mm.then_inc(score_ready, 1)
                        elif s[0] == "pT":
                            a = s[1]
                            pe.wait_ge(prob_done, HALVES * i + a + 1)
                            for n in range(BH // BT):
                                mm = nc.tensor.transpose(bank[:, n * P:(n + 1) * P], prob[:, a, n * BT:(n + 1) * BT, :].rearrange("p b s -> p (b s)"), sh.ident[:, :])
                        elif s[0] == "oT":
                            _, a, b = s
                            settled(("pT", a))
                            pe.wait_ge(v_done, i + 1)
                            rows = slice(b * S, (b + 1) * S)
                            for n in range(BH // BT):
                                mm = nc.tensor.matmul(bank[:, n * P:(n + 1) * P], v[rows, a * BH // BT + n], pT[rows, a, n * P:(n + 1) * P],
                                                      start=True, stop=True)
                        elif s[0] == "out":
                            t = s[1]
                            settled(("oT", t // (NT // 2), BT - 1))
                            if t == 0:
                                settled(("woT", G - 1))
                            at = slice(t * P, (t + 1) * P)
                            for g in range(G):
                                mm = three_passes(nc, bank[:, :], o_hi[:, g, at], o_lo[:, g, at], woT_hi[:, g], woT_lo[:, g], g == 0, g == G - 1)
                        if s in job:
                            mm.then_inc(ready, 1)


def route(nc, A, sh):
    with ExitStack() as ctx:
        def sb(name, shape, dt=F32):
            return ctx.enter_context(nc.sbuf_tensor("r_" + name, shape, dt))

        def sem(name):
            return ctx.enter_context(nc.semaphore("r_" + name))

        xn = sb("xn", [P, NT, D])
        xT = sb("xT", [P, 2, DCH, P])
        gate = sb("gate", [P, DCH, E])
        before, ones = sb("before", [P, P]), sb("ones", [P, P])
        order, slots = sb("order", [P, E]), sb("slots", [P, MAXSLOT])
        logit, pick, first, second, both = (sb(n, [P, NT, E]) for n in ("logit", "pick", "first", "second", "both"))
        rank, scan, scan2, place = (sb(n, [P, NT, E]) for n in ("rank", "scan", "scan2", "place"))
        best, top1, top2, ratio, den = (sb(n, [P, NT]) for n in ("best", "top1", "top2", "ratio", "den"))
        pos = sb("pos", [P, 2, NT])
        blocks, more, start, start2 = (sb(n, [P, E]) for n in ("blocks", "more", "start", "start2"))
        reach, expert = sb("reach", [P, MAXSLOT, E]), sb("expert", [P, MAXSLOT])
        ln = LayerNorm(nc, ctx, "r_ln")
        tr = [ctx.enter_context(nc.psum_tensor(f"r_tr{n}", [P, BANK], F32)) for n in range(2)]
        lg = ctx.enter_context(nc.psum_tensor("r_lg", [P, BANK], F32))
        rk = ctx.enter_context(nc.psum_tensor("r_rk", [P, BANK], F32))
        tt = ctx.enter_context(nc.psum_tensor("r_tt", [P, BANK], F32))

        const_in, ones_done, xn_done, ready, free = sem("const_in"), sem("ones_done"), sem("xn_done"), sem("ready"), sem("free")
        logits_ready, both_done, ranks_ready, gap_done, ratio_done = (
            sem(n) for n in ("logits_ready", "both_done", "ranks_ready", "gap_done", "ratio_done"))
        chain, pos_done, scattered = sem("chain"), sem("pos_done"), sem("scattered")

        with nc.Block() as block:
            @block.sync
            def _(sp):
                sp.dma_start(gate[:, :, :], A["gate_w"].rearrange("(c p) e -> p c e", p=P)).then_inc(const_in, 16)
                sp.dma_start(before[:, :], A["before"]).then_inc(const_in, 16)
                sp.dma_start(order[:, :], A["order"]).then_inc(const_in, 16)
                sp.dma_start(slots[:, :], A["slots"]).then_inc(const_in, 16)

            @block.gpsimd
            def _(pool):
                nc.gpsimd.memset(ones[:, :], 1.0).then_inc(ones_done, 1)
                pool.wait_ge(pos_done, 1)
                rows = sh.sorted_dram
                for t in range(NT):
                    for k in range(2):
                        pool.indirect_dma_start(rows, bass.IndirectOffsetOnAxis(ap=sh.pos[:, k, t:t + 1], axis=0), xn[:, t], None).then_inc(scattered, 16)
                pool.wait_ge(scattered, 16 * 2 * NT)

            @block.scalar
            def _(act):
                ln.take_root(act, 0, NT)
                act.wait_ge(gap_done, 1)
                nc.scalar.activation(ratio[:, :], top2[:, :], ACT.Exp).then_inc(ratio_done, 1)

            def logits(pe, t):
                pe.wait_ge(free, t + 1)
                for c in range(DCH):
                    mm = nc.tensor.matmul(lg[:, t * E:(t + 1) * E], xT[:, t % 2, c], gate[:, c], start=c == 0, stop=c == DCH - 1)
                return mm

            @block.tensor
            def _(pe):
                pe.wait_ge(const_in, 64)
                for t in range(NT):
                    pe.wait_ge(xn_done, t + 1)
                    if t >= 2:
                        pe.wait_ge(free, t - 1)
                    for c in range(DCH):
                        mm = nc.tensor.transpose(tr[t % 2][:, c * P:(c + 1) * P], xn[:, t, c * P:(c + 1) * P], sh.ident[:, :])
                    mm.then_inc(ready, 1)
                    if t >= 1:
                        logits(pe, t - 1)
                logits(pe, NT - 1).then_inc(logits_ready, 1)
                pe.wait_ge(both_done, 1)
                pe.wait_ge(ones_done, 1)
                flat = both[:, :, :].rearrange("p t e -> p (t e)")
                nc.tensor.matmul(rk[:, 0:NT * E], before[:, :], flat, start=True, stop=True)
                nc.tensor.matmul(tt[:, 0:NT * E], ones[:, :], flat, start=True, stop=True).then_inc(ranks_ready, 1)

            @block.vector
            def _(dve):
                v = nc.vector
                for t in range(NT):
                    ln.statistics(dve, sh.x[:, t], t)
                ln.variance(dve, 0, NT)
                ln.power(dve, 0, NT)
                for t in range(NT):
                    ln.apply(t, xn[:, t], sh.x[:, t]).then_inc(xn_done, 1)
                for t in range(NT):
                    dve.wait_ge(ready, t + 1)
                    v.tensor_copy(xT[:, t % 2].rearrange("p c t -> p (c t)"), tr[t % 2][:, :]).then_inc(free, 1)
                count = [0]

                def then(instruction):
                    instruction.then_inc(chain, 1)
                    count[0] += 1
                    dve.wait_ge(chain, count[0])

                def over_e(a):
                    return a.unsqueeze(2).to_broadcast([P, NT, E])

                order_b = order[:, :].unsqueeze(1).to_broadcast([P, NT, E])

                def choose(one_hot, top):
                    then(v.tensor_reduce(top[:, :], logit[:, :, :], AX, ALU.max))
                    then(v.tensor_tensor(pick[:, :, :], logit[:, :, :], over_e(top[:, :]), ALU.is_equal))
                    then(v.tensor_tensor(pick[:, :, :], pick[:, :, :], order_b, ALU.mult))
                    then(v.tensor_reduce(best[:, :], pick[:, :, :], AX, ALU.max))
                    then(v.tensor_tensor(one_hot[:, :, :], pick[:, :, :], over_e(best[:, :]), ALU.is_equal))

                dve.wait_ge(const_in, 64)
                dve.wait_ge(logits_ready, 1)
                then(v.tensor_copy(logit[:, :, :].rearrange("p t e -> p (t e)"), lg[:, 0:NT * E]))
                choose(first, top1)
                then(v.scalar_tensor_tensor(logit[:, :, :].rearrange("p t e -> p (t e)"), first[:, :, :].rearrange("p t e -> p (t e)"), MASKED,
                                            logit[:, :, :].rearrange("p t e -> p (t e)"), ALU.mult, ALU.add))
                choose(second, top2)
                v.tensor_tensor(both[:, :, :], first[:, :, :], second[:, :, :], ALU.add).then_inc(both_done, 1)
                v.tensor_tensor(top2[:, :], top2[:, :], top1[:, :], ALU.subtract).then_inc(gap_done, 1)
                dve.wait_ge(ratio_done, 1)
                then(v.tensor_scalar_add(den[:, :], ratio[:, :], 1.0))
                then(v.reciprocal(sh.weight[:, 0], den[:, :]))
                then(v.tensor_tensor(sh.weight[:, 1], ratio[:, :], sh.weight[:, 0], ALU.mult))
                dve.wait_ge(ranks_ready, 1)
                then(v.tensor_copy(scan[:, :, :].rearrange("p t e -> p (t e)"), tt[:, 0:NT * E]))
                a, b = scan, scan2
                for shift in (1, 2, 4):
                    v.tensor_copy(b[:, 0:shift], a[:, 0:shift])
                    then(v.tensor_tensor(b[:, shift:NT], a[:, shift:NT], a[:, 0:NT - shift], ALU.add))
                    a, b = b, a
                v.tensor_copy(rank[:, 0], rk[:, 0:E])
                then(v.tensor_tensor(rank[:, 1:NT].rearrange("p t e -> p (t e)"), rk[:, E:NT * E], a[:, 0:NT - 1].rearrange("p t e -> p (t e)"), ALU.add))
                load = a[:, NT - 1]
                then(v.tensor_scalar(blocks[:, :], load, float(CAP), 1.0, ALU.is_gt, ALU.add))
                for j in range(2, T // CAP):
                    then(v.tensor_scalar(more[:, :], load, float(j * CAP), None, ALU.is_gt))
                    then(v.tensor_tensor(blocks[:, :], blocks[:, :], more[:, :], ALU.add))
                then(v.tensor_copy(start[:, :], blocks[:, :]))
                a, b = start, start2
                for shift in (1, 2, 4):
                    v.tensor_copy(b[:, 0:shift], a[:, 0:shift])
                    then(v.tensor_tensor(b[:, shift:E], a[:, shift:E], a[:, 0:E - shift], ALU.add))
                    a, b = b, a
                v.tensor_copy(sh.table[:, MAXSLOT:MAXSLOT + 1], a[:, E - 1:E])
                then(v.tensor_tensor(b[:, :], a[:, :], blocks[:, :], ALU.subtract))
                begin = b
                then(v.scalar_tensor_tensor(place[:, :, :], begin[:, :].unsqueeze(1).to_broadcast([P, NT, E]), float(CAP), rank[:, :, :], ALU.mult, ALU.add))
                for k, one_hot in enumerate((first, second)):
                    then(v.tensor_tensor(pick[:, :, :], place[:, :, :], one_hot[:, :, :], ALU.mult))
                    then(v.tensor_reduce(pos[:, k], pick[:, :, :], AX, ALU.add))
                v.tensor_copy(sh.pos[:, :, :], pos[:, :, :]).then_inc(pos_done, 1)
                then(v.tensor_tensor(reach[:, :, :], slots[:, :].unsqueeze(2).to_broadcast([P, MAXSLOT, E]),
                                     begin[:, :].unsqueeze(1).to_broadcast([P, MAXSLOT, E]), ALU.is_ge))
                then(v.tensor_reduce(expert[:, :], reach[:, :, :], AX, ALU.add))
                then(v.tensor_scalar_add(sh.table[:, 0:MAXSLOT], expert[:, :], -1.0))


def expert_blocks(nc, A, sh):
    with ExitStack() as ctx:
        def sb(name, shape, dt=F32):
            return ctx.enter_context(nc.sbuf_tensor("f_" + name, shape, dt))

        def sem(name):
            return ctx.enter_context(nc.semaphore("f_" + name))

        UNITS = 4
        MU = M // UNITS
        PARTS = MU // P
        STEPS = M // P
        NRAW, NSPLIT, NHB, TK = 4, 2, 4, CAP // P
        w_raw = sb("w_raw", [P, NRAW, 3, DCH * MU])
        w_hi, w_lo = sb("w_hi", [P, NSPLIT, 3, DCH * MU], F32R), sb("w_lo", [P, NSPLIT, 3, DCH * MU], F32R)
        rows = sb("rows", [P, TK, D])
        xT_hi, xT_lo = sb("xT_hi", [P, 2, DCH, CAP], F32R), sb("xT_lo", [P, 2, DCH, CAP], F32R)
        gated, prod = sb("gated", [P, 2, CAP]), sb("prod", [P, 2, CAP])
        h_hi, h_lo = sb("h_hi", [P, 2, CAP], F32R), sb("h_lo", [P, 2, CAP], F32R)
        y = sb("y", [P, TK, D])
        hb = [ctx.enter_context(nc.psum_tensor(f"f_h{n}", [P, BANK], F32)) for n in range(NHB)]
        yb = [ctx.enter_context(nc.psum_tensor(f"f_y{n}", [P, BANK], F32)) for n in range(TK)]
        tb = [ctx.enter_context(nc.psum_tensor(f"f_t{n}", [P, BANK], F32)) for n in range(TK)]

        raw_in = [sem(f"raw_in{q}") for q in range(NRAW)]
        hi_ready, split_ready, unit_used = sem("hi_ready"), sem("split_ready"), sem("unit_used")
        rows_in, t_ready, t_hi, t_done = sem("rows_in"), sem("t_ready"), sem("t_hi"), sem("t_done")
        h_ready, silu_done, prod_done, h_hi_done, h_done = (sem(n) for n in ("h_ready", "silu_done", "prod_done", "h_hi_done", "h_done"))
        y_free, y_out, drained = sem("y_free"), sem("y_out"), sem("drained")
        CREDIT = 3 * NRAW

        w0_d = A["w0"].rearrange("e (c p) (u m) -> e u p c m", p=P, u=UNITS)
        w1_d = A["w1"].rearrange("e (c p) (u m) -> e u p c m", p=P, u=UNITS)
        wo_d = A["ffn_wo"].rearrange("e (u q p) d -> e u p q d", p=P, u=UNITS)
        rows_d = sh.sorted_dram.rearrange("(i k p) d -> i p k d", k=TK, p=P)
        y_d = sh.y_dram.rearrange("(i k p) d -> i p k d", k=TK, p=P)

        with nc.Block() as block:
            def slots_of(eng):
                return eng.value_load(sh.table[0:1, MAXSLOT:MAXSLOT + 1], min_val=E, max_val=MAXSLOT - 1)

            @block.sync
            def _(sp):
                n_slots = slots_of(sp)
                all_rows, all_units = sp.snap(16 * (n_slots + 1)), sp.snap(48 * (n_slots + 1))

                def load_unit(e, u, n):
                    sp.wait_ge(split_ready, 3 * n + 3)
                    for m, src in enumerate((w0_d, w1_d)):
                        sp.dma_start(w_raw[:, u, m].rearrange("p (c m) -> p c m", c=DCH), src[e, u]).then_inc(raw_in[u], 16)
                    sp.dma_start(w_raw[:, u, 2].rearrange("p (q d) -> p q d", q=PARTS), wo_d[e, u]).then_inc(raw_in[u], 16)

                sp.dma_start(rows[:, :, :], rows_d[0]).then_inc(rows_in, 16)
                for u in range(UNITS):
                    load_unit(0, u, u)
                with sp.Fori(0, n_slots) as i:
                    e = sp.value_load(sh.table[0:1, bass.ds(i + 1, 1)], min_val=0, max_val=E - 1)
                    sp.wait_ge(t_ready, TK * (i + 1))
                    sp.dma_start(rows[:, :, :], rows_d[i + 1]).then_inc(rows_in, 16)
                    for u in range(UNITS):
                        load_unit(e, u, UNITS * (i + 1) + u)
                    sp.wait_ge(y_free, i + 2)
                    sp.dma_start(y_d[i], y[:, :, :]).then_inc(y_out, 16)
                for sem_in, value in [(y_out, all_rows)] + [(raw_in[u], all_units) for u in range(UNITS)] + [(rows_in, all_rows)]:
                    sp.wait_ge(sem_in, value)
                    sp.sem_inc(drained, 1)

            @block.scalar
            def _(act):
                n_slots = slots_of(act)

                def unit_hi(u, m, n, loads):
                    act.wait_ge(raw_in[u], 48 * loads)
                    act.wait_ge(unit_used, n + 1)
                    nc.scalar.copy(w_hi[:, u % NSPLIT, m], w_raw[:, u, m]).then_inc(hi_ready, 1)

                def tokens_hi(slot, par):
                    for k in range(TK):
                        act.wait_ge(t_ready, TK * slot + k + 1)
                        out = xT_hi[:, bass.ds(par, 1), :, k * P:(k + 1) * P].rearrange("p o c t -> p (o c) t")
                        nc.scalar.copy(out, tb[k][:, :].rearrange("p (c t) -> p c t", c=DCH)).then_inc(t_hi, 1)

                tokens_hi(0, 0)
                for m in range(3):
                    unit_hi(0, m, 0, 1)
                with act.Fori(0, n_slots) as i:
                    for j in range(STEPS):
                        u = (j // PARTS + 1) % UNITS
                        n, loads = UNITS * i + j // PARTS + 1, i + 1 + (j // PARTS + 1) // UNITS
                        act.wait_ge(h_ready, STEPS * i + j + 1)
                        nc.scalar.activation(gated[:, j % 2], hb[j % NHB][:, 0:CAP], ACT.Silu).then_inc(silu_done, 1)
                        act.wait_ge(prod_done, NHB + STEPS * i + j + 1)
                        nc.scalar.copy(h_hi[:, j % 2], prod[:, j % 2]).then_inc(h_hi_done, 1)
                        for m in ((0, 1) if j % PARTS == 0 else (2,)):
                            unit_hi(u, m, n, loads)
                    tokens_hi(i + 1, (i + 1) & 1)

            @block.vector
            def _(dve):
                n_slots = slots_of(dve)
                dve.sem_inc(split_ready, CREDIT)
                dve.sem_inc(prod_done, NHB)
                dve.sem_inc(y_free, 1)
                dve.sem_inc(y_out, 16)

                def unit_lo(u, m, n):
                    dve.wait_ge(hi_ready, 3 * n + m + 1)
                    split_lo(nc, w_lo[:, u % NSPLIT, m], w_raw[:, u, m], w_hi[:, u % NSPLIT, m]).then_inc(split_ready, 1)

                def tokens_lo(slot, par):
                    for k in range(TK):
                        dve.wait_ge(t_hi, TK * slot + k + 1)
                        at = [x[:, bass.ds(par, 1), :, k * P:(k + 1) * P].rearrange("p o c t -> p (o c) t") for x in (xT_hi, xT_lo)]
                        split_lo(nc, at[1], tb[k][:, :].rearrange("p (c t) -> p c t", c=DCH), at[0]).then_inc(t_done, 1)

                tokens_lo(0, 0)
                for m in range(3):
                    unit_lo(0, m, 0)
                with dve.Fori(0, n_slots) as i:
                    for j in range(STEPS):
                        u, n = (j // PARTS + 1) % UNITS, UNITS * i + j // PARTS + 1
                        dve.wait_ge(silu_done, STEPS * i + j + 1)
                        nc.vector.tensor_tensor(prod[:, j % 2], hb[j % NHB][:, CAP:2 * CAP], gated[:, j % 2], ALU.mult).then_inc(prod_done, 1)
                        dve.wait_ge(h_hi_done, STEPS * i + j + 1)
                        split_lo(nc, h_lo[:, j % 2], prod[:, j % 2], h_hi[:, j % 2]).then_inc(h_done, 1)
                        for m in ((0, 1) if j % PARTS == 0 else (2,)):
                            unit_lo(u, m, n)
                    tokens_lo(i + 1, (i + 1) & 1)
                    dve.wait_ge(unit_used, NSPLIT + UNITS * (i + 1))
                    dve.wait_ge(y_out, 16 * (i + 1))
                    for k in range(TK):
                        cp = nc.vector.tensor_copy(y[:, k], yb[k][:, :])
                    cp.then_inc(y_free, 1)

            @block.tensor
            def _(pe):
                n_slots = slots_of(pe)
                pe.sem_inc(unit_used, NSPLIT)

                def transposes(slot):
                    pe.wait_ge(rows_in, 16 * (slot + 1))
                    for k in range(TK):
                        for c in range(DCH):
                            mm = nc.tensor.transpose(tb[k][:, c * P:(c + 1) * P], rows[:, k, c * P:(c + 1) * P], sh.ident[:, :])
                        mm.then_inc(t_ready, 1)

                def down(i, j):
                    s, q = j // PARTS % NSPLIT, j % PARTS
                    pe.wait_ge(h_done, STEPS * i + j + 1)
                    if q == 0:
                        pe.wait_ge(split_ready, CREDIT + 3 * (UNITS * i + j // PARTS) + 3)
                    if j == 0:
                        pe.wait_ge(y_free, i + 1)
                    for k in range(TK):
                        at, w = slice(k * P, (k + 1) * P), slice(q * D, (q + 1) * D)
                        mm = three_passes(nc, yb[k][:, :], h_hi[:, j % 2, at], h_lo[:, j % 2, at], w_hi[:, s, 2, w], w_lo[:, s, 2, w],
                                          j == 0, j == STEPS - 1)
                    if q == PARTS - 1:
                        mm.then_inc(unit_used, 1)

                transposes(0)
                with pe.Fori(0, n_slots) as i:
                    par = i & 1
                    for j in range(STEPS):
                        s, q = j // PARTS % NSPLIT, j % PARTS
                        if j == 0:
                            pe.wait_ge(t_done, TK * (i + 1))
                        if q == 0:
                            pe.wait_ge(split_ready, CREDIT + 3 * (UNITS * i + j // PARTS) + 2)
                        pe.wait_ge(prod_done, STEPS * i + j + 1)
                        for m in range(2):
                            for c in range(DCH):
                                w = slice(c * MU + q * P, c * MU + (q + 1) * P)
                                x = [t[:, bass.ds(par, 1), c, :].rearrange("p o t -> p (o t)") for t in (xT_hi, xT_lo)]
                                mm = three_passes(nc, hb[j % NHB][:, m * CAP:(m + 1) * CAP], w_hi[:, s, m, w], w_lo[:, s, m, w], x[0], x[1],
                                                  c == 0, c == DCH - 1)
                        mm.then_inc(h_ready, 1)
                        if j:
                            down(i, j - 1)
                    transposes(i + 1)
                    down(i, STEPS - 1)


def combine(nc, A, sh):
    with ExitStack() as ctx:
        got = ctx.enter_context(nc.sbuf_tensor("c_got", [P, NT, 2, D], F32))
        got_in = [ctx.enter_context(nc.semaphore(f"c_got_in{t}")) for t in range(NT)]
        half, done, stored = (ctx.enter_context(nc.semaphore(n)) for n in ("c_half", "c_done", "c_stored"))
        with nc.Block() as block:
            @block.gpsimd
            def _(pool):
                for t in range(NT):
                    for k in range(2):
                        pool.indirect_dma_start(got[:, t, k], None, sh.y_dram, bass.IndirectOffsetOnAxis(ap=sh.pos[:, k, t:t + 1], axis=0)).then_inc(got_in[t], 16)

            @block.vector
            def _(dve):
                for t in range(NT):
                    dve.wait_ge(got_in[t], 32)
                    for k in range(2):
                        ins = nc.vector.scalar_tensor_tensor(sh.x[:, t], got[:, t, k], sh.weight[:, k, t:t + 1], sh.x[:, t], ALU.mult, ALU.add)
                        if k == 0:
                            ins.then_inc(half, 1)
                            dve.wait_ge(half, t + 1)
                    ins.then_inc(done, 1)

            @block.sync
            def _(sp):
                out = A["out"].rearrange("b s d -> (b s) d").rearrange("(n p) d -> n p d", p=P)
                for t in range(NT):
                    sp.wait_ge(done, t + 1)
                    sp.dma_start(out[t], sh.x[:, t]).then_inc(stored, 16)
                sp.wait_ge(stored, 16 * NT)


def decoder_layer(nc, A):
    with ExitStack() as ctx:
        def sb(where, name, shape, dt=F32):
            return where.enter_context(nc.sbuf_tensor(name, shape, dt))

        sh = Shared()
        sh.last_dram = nc.dram_tensor("last_keys", (B, DC), F32, kind="Internal").ap()
        sh.ctx_dram = nc.dram_tensor("ctx_out", (NT, P, H * P), F32, kind="Internal").ap()
        sh.sorted_dram = nc.dram_tensor("sorted_rows", (MAXSLOT * CAP, D), F32, kind="Internal").ap()
        sh.y_dram = nc.dram_tensor("expert_rows", (MAXSLOT * CAP, D), F32, kind="Internal").ap()
        sh.ident = sb(ctx, "ident", [P, P])
        with ExitStack() as cross:
            def pair(name, shape):
                return [sb(cross, f"{name}_{part}", shape, F32R) for part in ("hi", "lo")]

            sh.m1_hi, sh.m1_lo = pair("m1", [P, DCH, H * R])
            sh.xT_hi, sh.xT_lo = pair("xT", [P, DCH, T])
            sh.krT_hi, sh.krT_lo = pair("krT", [P, H, P])
            sh.lastT_hi, sh.lastT_lo = pair("lastT", [P, B])
            prepare(nc, A, sh)
            cross_attention(nc, A, sh)
        sh.x = sb(ctx, "x_res", [P, NT, D])
        sh.pos = sb(ctx, "pos", [P, 2, NT], I32)
        sh.weight = sb(ctx, "weight", [P, 2, NT])
        sh.table = sb(ctx, "table", [P, MAXSLOT + 1], I32)
        project_context(nc, A, sh)
        self_attention(nc, A, sh)
        route(nc, A, sh)
        expert_blocks(nc, A, sh)
        combine(nc, A, sh)


def shape_tables():
    f = np.float32
    inv = (f(1.0) / np.power(f(10000.0), np.arange(0, DC, 2, dtype=f) / f(DC))).astype(f)
    freqs = np.arange(L, dtype=f)[:, None] * inv[None, :]
    cos, sin = np.repeat(np.cos(freqs), 2, axis=-1).astype(f), np.repeat(np.sin(freqs), 2, axis=-1).astype(f)
    sin[:, :DC // 2] *= -1
    cut = {n: np.ascontiguousarray(t[:LC * P].reshape(LC, P, DC).transpose(1, 0, 2)) for n, t in (("cos", cos), ("sin", sin))}
    t, s = np.arange(S)[:, None], np.arange(S)[None, :]
    mask = np.tile(np.where((s <= t) & ((s < 4) | (s >= t - 64 + 1)), f(0), f(MASKED)).astype(f), (G, 1))
    before = (np.arange(P)[:, None] < np.arange(P)[None, :]).astype(f)
    return {
        "ident": np.eye(P, dtype=f), "cos": cut["cos"], "sin": cut["sin"],
        "last_cos": np.tile(cos[L - 1:], (B, 1)), "last_sin": np.tile(sin[L - 1:], (B, 1)),
        "mask": mask, "before": before,
        "order": np.tile(np.arange(E, 0, -1).astype(f), (P, 1)),
        "slots": np.tile(np.arange(MAXSLOT).astype(f), (P, 1)),
    }


INPUTS = {"x": "x", "ctx_512": "ctx", "L0_xattn_Wq": "Wq", "L0_xattn_w_kc_q": "w_kc_q", "L0_xattn_w_kc_kv": "w_kc_kv",
          "L0_xattn_W_qr": "W_qr", "L0_xattn_W_kr": "W_kr", "L0_xattn_Wo": "Wo", "L0_attn_wq": "wq", "L0_attn_wk": "wk",
          "L0_attn_wv": "wv", "L0_attn_wo": "wo", "L0_ffn_gate_w": "gate_w", "L0_ffn_w0": "w0", "L0_ffn_w1": "w1",
          "L0_ffn_wo": "ffn_wo"}


def kernel(**inputs):
    import concourse.bacc as bacc
    from concourse.bass_utils import run_bass_kernel_spmd

    nc = bacc.Bacc("TRN2", target_bir_lowering=False, num_devices=1)
    arrays = {f"in_{short}": np.ascontiguousarray(inputs[name]) for name, short in INPUTS.items()}
    arrays |= {f"in_{name}": a for name, a in shape_tables().items()}
    A = {name[3:]: nc.dram_tensor(name, a.shape, mybir.dt.from_np(a.dtype), kind="ExternalInput").ap() for name, a in arrays.items()}
    A["out"] = nc.dram_tensor("out", (B, S, D), F32, kind="ExternalOutput").ap()
    decoder_layer(nc, A)
    return run_bass_kernel_spmd(nc, [arrays], core_ids=[0]).results[0]["out"]
```

```python
from contextlib import ExitStack


import numpy as np

import concourse.bass as bass
from concourse import mybir

F32 = mybir.dt.float32
F32R = mybir.dt.float32r
I32 = mybir.dt.int32
U32 = mybir.dt.uint32
ALU = mybir.AluOpType
ACT = mybir.ActivationFunctionType
AX = mybir.AxisListType.X

P = 128
B, S, D = 32, 32, 512
L, DC = 257, 128
H, R, DCQ = 16, 64, 384
KVH, G = 4, 4
E, M = 8, 1024
T = B * S
NT = T // P
BT = P // S
DCH = D // P
LC = L // P
LP = L + 1
BANK = 512
EPS = 1e-5
SG = 4
GB = B // SG
GT = T // SG
MINTILE = 2
MAXTILE = MINTILE * E + 2 * T // P
MASKED = -3.0e38


class Shared:
    pass


def split_lo(nc, out, value, hi):
    return nc.vector.tensor_tensor(out, value, hi.bitcast(F32), ALU.subtract)


def three_passes(nc, out, lhs_hi, lhs_lo, rhs_hi, rhs_lo, first, last):
    nc.tensor.matmul(out, lhs_lo, rhs_hi, start=first, stop=False)
    nc.tensor.matmul(out, lhs_hi, rhs_lo, start=False, stop=False)
    return nc.tensor.matmul(out, lhs_hi, rhs_hi, start=False, stop=last)


def numbered(steps, kinds):
    return {s: n for n, s in enumerate([s for s in steps if s[0] in kinds])}


class LayerNorm:

    def __init__(self, nc, ctx, name):
        def sb(what, shape):
            return ctx.enter_context(nc.sbuf_tensor(f"{name}_{what}", shape, F32))

        self.nc = nc
        self.stats, self.mv = sb("stats", [P, NT, 6]), sb("mv", [P, NT, 2])
        self.var, self.root, self.inv, self.corr, self.rstd = (sb(n, [P, NT]) for n in ("var", "root", "inv", "corr", "rstd"))
        self.stats_done, self.var_done, self.root_done, self.chain = (
            ctx.enter_context(nc.semaphore(f"{name}_{n}")) for n in ("stats_done", "var_done", "root_done", "chain"))
        self.chain_n = self.ranges = self.roots = 0

    def step(self, dve, instruction):
        instruction.then_inc(self.chain, 1)
        self.chain_n += 1
        dve.wait_ge(self.chain, self.chain_n)

    def statistics(self, x, t):
        self.nc.vector.bn_stats(self.stats[:, bass.ds(t, 1)].rearrange("p o s -> p (o s)"), x).then_inc(self.stats_done, 1)

    def variance(self, dve, t0, t1):
        dve.wait_ge(self.stats_done, t1)
        for t in range(t0, t1):
            last = self.nc.vector.bn_aggr(self.mv[:, t], self.stats[:, t])
        self.step(dve, last)
        self.nc.vector.tensor_scalar_add(self.var[:, t0:t1], self.mv[:, t0:t1, 1], EPS).then_inc(self.var_done, 1)

    def take_root(self, act, t0, t1):
        self.roots += 1
        act.wait_ge(self.var_done, self.roots)
        self.nc.scalar.activation(self.root[:, t0:t1], self.var[:, t0:t1], ACT.Sqrt).then_inc(self.root_done, 1)

    def power(self, dve, t0, t1):
        v, var, inv, corr = self.nc.vector, self.var[:, t0:t1], self.inv[:, t0:t1], self.corr[:, t0:t1]
        self.ranges += 1
        dve.wait_ge(self.root_done, self.ranges)
        self.step(dve, v.reciprocal(inv, self.root[:, t0:t1]))
        self.step(dve, v.tensor_tensor(corr, inv, inv, ALU.mult))
        self.step(dve, v.tensor_tensor(corr, corr, var, ALU.mult))
        self.step(dve, v.tensor_scalar(corr, corr, -0.5, 1.5, ALU.mult, ALU.add))
        self.step(dve, v.tensor_tensor(self.rstd[:, t0:t1], inv, corr, ALU.mult))

    def apply(self, t, out, x):
        return self.nc.vector.tensor_scalar(out, x, self.mv[:, t, 0:1], self.rstd[:, t:t + 1], ALU.subtract, ALU.mult)


def prepare(nc, A, sh):
    HG = 4
    NG = H // HG
    with ExitStack() as ctx:
        def sb(name, shape, dt=F32):
            return ctx.enter_context(nc.sbuf_tensor("p_" + name, shape, dt))

        def sem(name):
            return ctx.enter_context(nc.semaphore("p_" + name))

        x = sb("x", [P, NT, D])
        xn = sb("xn", [P, 2, D])
        ln = LayerNorm(nc, ctx, "p_ln")
        kcq = sb("kcq", [P, 2, HG, DCQ])
        kcqT = sb("kcqT", [P, 2, DCQ // P, HG, P])
        wq = sb("wq", [P, 2, HG, D])
        wqr = sb("wqr", [P, DCQ // P, H, R])
        m2 = sb("m2", [P, 2, HG, R])
        wkr = sb("wkr", [P, H, R])
        last = sb("last", [B, DC])
        last_cos, last_sin = sb("last_cos", [B, DC]), sb("last_sin", [B, DC])
        last_rot = sb("last_rot", [B, DC])
        last_a, last_b = sb("last_a", [B, DC]), sb("last_b", [B, DC])
        NB = 8
        ring = [ctx.enter_context(nc.psum_tensor(f"p_ring{n}", [P, BANK], F32)) for n in range(NB)]

        ident_in, wqr_in, wkr_in, last_in = (sem(n) for n in ("ident_in", "wqr_in", "wkr_in", "last_in"))
        x_in = [sem("x_in0"), sem("x_in1")]
        kcq_in, wq_in = [sem("kcq_in0"), sem("kcq_in1")], [sem("wq_in0"), sem("wq_in1")]
        ready, hi_done, free = sem("ready"), sem("hi"), sem("free")
        zeroed = sem("zeroed")
        xn_done, dve_chain, last_done, last_out = sem("xn_done"), sem("dve_chain"), sem("last_done"), sem("last_out")

        def group(g):
            return [("m2", g), ("m1", g, 0), ("m1", g, 1)] + [("kcqT", g + 1, q) for q in range(DCQ // P)]

        steps = [("kcqT", 0, q) for q in range(DCQ // P)] + group(0) + [("xT", 0), ("xT", 1)] + group(1) + [("xT", 2), ("xT", 3)]
        steps += group(2) + [("krT", 0), ("krT", 1), ("xT", 4), ("m2", NG - 1), ("xT", 5), ("xT", 6), ("xT", 7), ("lastT",)]
        steps += [("m1", NG - 1, 0), ("m1", NG - 1, 1)]
        job = {s: n for n, s in enumerate(steps)}
        split = numbered(steps, ("xT", "m1", "krT", "lastT"))

        with nc.Block() as block:
            @block.sync
            def _(sp):
                sp.dma_start(sh.ident[:, :], A["ident"]).then_inc(ident_in, 16)
                kcq_d = A["w_kc_q"].rearrange("(g h) k q -> g k h q", h=HG)
                wq_d = A["Wq"].rearrange("(g h k) d -> g k h d", h=HG, k=P)
                x_d = A["x"].rearrange("b s d -> (b s) d").rearrange("(n p) d -> p n d", p=P)
                sp.dma_start(kcq[:, 0], kcq_d[0]).then_inc(kcq_in[0], 16)
                for c in range(DCQ // P):
                    sp.dma_start(wqr[:, c], A["W_qr"][:, c * P:(c + 1) * P, :].rearrange("h q r -> q h r")).then_inc(wqr_in, 16)
                sp.dma_start(x[:, 0:NT // 2], x_d[:, 0:NT // 2]).then_inc(x_in[0], 16)
                sp.dma_start(wq[:, 0], wq_d[0]).then_inc(wq_in[0], 16)
                sp.dma_start(kcq[:, 1], kcq_d[1]).then_inc(kcq_in[1], 16)
                sp.dma_start(x[:, NT // 2:], x_d[:, NT // 2:]).then_inc(x_in[1], 16)
                sp.dma_start(wq[:, 1], wq_d[1]).then_inc(wq_in[1], 16)
                sp.dma_start(last[:, :], A["ctx"][:, L - 1, :]).then_inc(last_in, 16)
                sp.dma_start(last_cos[:, :], A["last_cos"]).then_inc(last_in, 16)
                sp.dma_start(last_sin[:, :], A["last_sin"]).then_inc(last_in, 16)
                sp.dma_start(wkr[:, :, :], A["W_kr"].rearrange("h c r -> c h r")).then_inc(wkr_in, 16)
                for g in range(2, NG):
                    sp.wait_ge(ready, job["kcqT", g - 2, 2] + 1)
                    sp.dma_start(kcq[:, g % 2], kcq_d[g]).then_inc(kcq_in[g % 2], 16)
                    sp.wait_ge(ready, job["m1", g - 2, 1] + 1)
                    sp.dma_start(wq[:, g % 2], wq_d[g]).then_inc(wq_in[g % 2], 16)
                sp.wait_ge(last_done, 1)
                sp.dma_start(sh.last_dram, last_rot[:, :]).then_inc(last_out, 16)
                sp.wait_ge(last_out, 16)

            @block.gpsimd
            def _(pool):
                nc.gpsimd.memset(sh.krT_hi[:, :, :].bitcast(F32), 0.0).then_inc(zeroed, 1)
                nc.gpsimd.memset(sh.krT_lo[:, :, :].bitcast(F32), 0.0).then_inc(zeroed, 1)

            @block.scalar
            def _(act):
                for s in steps:
                    if s == ("m1", 0, 0):
                        ln.take_root(act, 0, NT // 2)
                    if s == ("m1", 1, 0):
                        ln.take_root(act, NT // 2, NT)
                    if s not in split:
                        continue
                    n = job[s]
                    bank = ring[n % NB]
                    act.wait_ge(ready, n + 1)
                    if s[0] == "xT":
                        out = sh.xT_hi[:, :, s[1] * P:(s[1] + 1) * P]
                        nc.scalar.copy(out, bank[:, :].rearrange("p (c t) -> p c t", c=DCH)).then_inc(hi_done, 1)
                    elif s[0] == "m1":
                        _, g, c = s
                        out = sh.m1_hi[:, 2 * c:2 * c + 2, g * HG * R:(g + 1) * HG * R]
                        nc.scalar.copy(out, bank[:, :].rearrange("p (c r) -> p c r", c=2)).then_inc(hi_done, 1)
                    elif s[0] == "krT":
                        act.wait_ge(zeroed, 2)
                        for e in range(2):
                            rows, heads = slice(R * e, R * e + R), slice(8 * s[1] + e, 8 * s[1] + 8, 2)
                            cp = nc.scalar.copy(sh.krT_hi[rows, heads, :], bank[rows, :].rearrange("p (j c) -> p j c", j=4))
                        cp.then_inc(hi_done, 1)
                    else:
                        nc.scalar.copy(sh.lastT_hi[:, :], bank[:, 0:B]).then_inc(hi_done, 1)

            @block.vector
            def _(dve):
                def rotate_last():
                    dve.wait_ge(last_in, 48)
                    nc.vector.tensor_tensor(last_a[:, :], last[:, :], last_cos[:, :], ALU.mult).then_inc(dve_chain, 1)
                    nc.vector.tensor_tensor(last_b[:, 0:64], last[:, 64:128], last_sin[:, 0:64], ALU.mult).then_inc(dve_chain, 1)
                    nc.vector.tensor_tensor(last_b[:, 64:128], last[:, 0:64], last_sin[:, 64:128], ALU.mult).then_inc(dve_chain, 1)
                    dve.wait_ge(dve_chain, 3)
                    nc.vector.tensor_tensor(last_rot[:, :], last_a[:, :], last_b[:, :], ALU.add).then_inc(last_done, 1)

                def norm_range(t0, t1):
                    dve.wait_ge(x_in[t0 // (NT // 2)], 16)
                    for t in range(t0, t1):
                        ln.statistics(x[:, t], t)
                    ln.variance(dve, t0, t1)
                    ln.power(dve, t0, t1)

                def norm(t):
                    if t >= 2:
                        dve.wait_ge(ready, job["xT", t - 2] + 1)
                    ln.apply(t, xn[:, t % 2], x[:, t]).then_inc(xn_done, 1)

                for s in steps:
                    if s == ("xT", NT - 1):
                        rotate_last()
                    n = job[s]
                    bank = ring[n % NB]
                    if s in split:
                        dve.wait_ge(hi_done, split[s] + 1)
                    else:
                        dve.wait_ge(ready, n + 1)
                    if s[0] == "kcqT":
                        _, g, q = s
                        nc.vector.tensor_copy(kcqT[:, g % 2, q].rearrange("p h k -> p (h k)"), bank[:, :]).then_inc(free, 1)
                    elif s[0] == "m2":
                        g = s[1]
                        nc.vector.tensor_copy(m2[:, g % 2].rearrange("p h r -> p (h r)"), bank[:, 0:HG * R]).then_inc(free, 1)
                        if g == 0:
                            norm_range(0, NT // 2)
                            norm(0)
                            norm(1)
                        elif g == 1:
                            norm_range(NT // 2, NT)
                    elif s[0] == "xT":
                        at = slice(s[1] * P, (s[1] + 1) * P)
                        split_lo(nc, sh.xT_lo[:, :, at], bank[:, :].rearrange("p (c t) -> p c t", c=DCH), sh.xT_hi[:, :, at]).then_inc(free, 1)
                        if s[1] + 2 < NT:
                            norm(s[1] + 2)
                    elif s[0] == "m1":
                        _, g, c = s
                        at = slice(g * HG * R, (g + 1) * HG * R)
                        split_lo(nc, sh.m1_lo[:, 2 * c:2 * c + 2, at], bank[:, :].rearrange("p (c r) -> p c r", c=2),
                                 sh.m1_hi[:, 2 * c:2 * c + 2, at]).then_inc(free, 1)
                    elif s[0] == "krT":
                        for e in range(2):
                            rows, heads = slice(R * e, R * e + R), slice(8 * s[1] + e, 8 * s[1] + 8, 2)
                            lo = split_lo(nc, sh.krT_lo[rows, heads, :], bank[rows, :].rearrange("p (j c) -> p j c", j=4), sh.krT_hi[rows, heads, :])
                        lo.then_inc(free, 1)
                    else:
                        split_lo(nc, sh.lastT_lo[:, :], bank[:, 0:B], sh.lastT_hi[:, :]).then_inc(free, 1)

            @block.tensor
            def _(pe):
                pe.wait_ge(ident_in, 16)
                for s in steps:
                    n = job[s]
                    bank = ring[n % NB]
                    if n >= NB:
                        pe.wait_ge(free, n - NB + 1)
                    if s[0] == "kcqT":
                        _, g, q = s
                        pe.wait_ge(kcq_in[g % 2], 16 * (g // 2 + 1))
                        for h in range(HG):
                            mm = nc.tensor.transpose(bank[:, h * P:(h + 1) * P], kcq[:, g % 2, h, q * P:(q + 1) * P], sh.ident[:, :])
                    elif s[0] == "m2":
                        g = s[1]
                        pe.wait_ge(wqr_in, 48)
                        pe.wait_ge(free, job["kcqT", g, 2] + 1)
                        for h in range(HG):
                            for q in range(3):
                                mm = nc.tensor.matmul(bank[:, h * R:(h + 1) * R], kcqT[:, g % 2, q, h, :], wqr[:, q, g * HG + h, :],
                                                      start=q == 0, stop=q == 2)
                    elif s[0] == "m1":
                        _, g, c = s
                        pe.wait_ge(wq_in[g % 2], 16 * (g // 2 + 1))
                        pe.wait_ge(free, job["m2", g] + 1)
                        for cc in range(2):
                            for h in range(HG):
                                mm = nc.tensor.matmul(bank[:, (cc * HG + h) * R:(cc * HG + h + 1) * R],
                                                      wq[:, g % 2, h, (2 * c + cc) * P:(2 * c + cc + 1) * P], m2[:, g % 2, h, :],
                                                      start=True, stop=True)
                    elif s[0] == "xT":
                        pe.wait_ge(xn_done, s[1] + 1)
                        for c in range(DCH):
                            mm = nc.tensor.transpose(bank[:, c * P:(c + 1) * P], xn[:, s[1] % 2, c * P:(c + 1) * P], sh.ident[:, :])
                    elif s[0] == "krT":
                        pe.wait_ge(wkr_in, 16)
                        for j in range(4):
                            h = 2 * (4 * s[1] + j)
                            mm = nc.tensor.transpose(bank[:, j * P:(j + 1) * P], wkr[:, h:h + 2, :].rearrange("p h r -> p (h r)"), sh.ident[:, :])
                    else:
                        pe.wait_ge(last_done, 1)
                        mm = nc.tensor.transpose(bank[:, 0:B], last_rot[:, :], sh.ident[0:B, 0:B])
                    mm.then_inc(ready, 1)


def cross_attention(nc, A, sh):
    with ExitStack() as ctx:
        def sb(name, shape, dt=F32):
            return ctx.enter_context(nc.sbuf_tensor("x_" + name, shape, dt))

        def sem(name):
            return ctx.enter_context(nc.semaphore("x_" + name))

        NQ = 4
        PAIRS = H // 2
        cos, sin = sb("cos", [P, LC, DC]), sb("sin", [P, LC, DC])
        qr_hi, qr_lo = sb("qr_hi", [P, NQ, GT], F32R), sb("qr_lo", [P, NQ, GT], F32R)
        qp_hi, qp_lo = sb("qp_hi", [P, GB, H, S], F32R), sb("qp_lo", [P, GB, H, S], F32R)
        raw = sb("raw", [P, 2, BT, LC, DC])
        rot = sb("rot", [P, BT, LC, DC])
        half = sb("half", [P, BT, LC, DC])
        kv_hi, kv_lo = sb("kv_hi", [P, 2, BT, LC, DC], F32R), sb("kv_lo", [P, 2, BT, LC, DC], F32R)
        kT_hi, kT_lo = sb("kT_hi", [P, 2, BT, LP], F32R), sb("kT_lo", [P, 2, BT, LP], F32R)
        last = sb("last", [1, GB, DC])
        attn = sb("attn", [P, 3, 4, L])
        aT_hi, aT_lo = sb("aT_hi", [P, LC, BANK], F32R), sb("aT_lo", [P, LC, BANK], F32R)
        aT_last = sb("aT_last", [1, BANK])
        negmax, total, recip = (sb(n, [P, 3, 4]) for n in ("negmax", "total", "recip"))
        out, out_done = sh.ctx_tile, sh.ctx_stored
        zero = sb("zero", [P, D])

        NB = 4
        ring = [ctx.enter_context(nc.psum_tensor(f"x_ring{n}", [P, BANK], F32)) for n in range(NB)]
        score = [ctx.enter_context(nc.psum_tensor(f"x_score{n}", [P, BANK], F32)) for n in range(4)]

        table_in, raw_in, last_in = sem("table_in"), [sem("raw_in0"), sem("raw_in1")], sem("last_in")
        rot_done, nat_hi, kv_done, raw_free = sem("rot_done"), sem("nat_hi"), sem("kv_done"), sem("raw_free")
        ready, hi_done, free = sem("ready"), sem("hi"), sem("free")
        score_ready, max_done, exp_done = sem("score_ready"), sem("max_done"), sem("exp_done")
        recip_done, norm_done = sem("recip_done"), sem("norm_done")
        pad_done, zero_done, zero_out = sem("pad_done"), sem("zero_done"), sem("zero_out")

        AHEAD, LAG = 2, 2
        steps = []
        for j in range(PAIRS):
            steps += [("qp", j)] + ([("qr", j + AHEAD)] if j + AHEAD < PAIRS else [])
            if j == 1:
                steps += [("kT", 0, c) for c in range(LC)] + [("kv", 0)]
        steps += [("kv", 1)]
        for b in range(GB + LAG):
            if b >= LAG:
                steps += [("aT", b - LAG, c) for c in (LC, *range(LC))]
            if b < GB:
                steps += [("sc", b)] + ([("kT", 1, c) for c in range(LC)] if b == 1 else [])
            elif b == GB + LAG - 1:
                steps += [("qr", 0), ("qr", 1)]
            if b >= LAG:
                steps += [("av", b - LAG)]
            if b < GB:
                steps += [("rc", b)]
        kinds = ("qr", "qp", "kT", "aT", "av")
        splits = ("qr", "qp", "kT")
        job = {s: n + AHEAD + 1 for n, s in enumerate([s for s in steps if s[0] in kinds])}
        split = {s: n + AHEAD for n, s in enumerate([s for s in job if s[0] in splits or (s[0] == "aT" and s[2] < LC)])}
        NJ, NS = len(job), len(split)

        def tokens_of(s, i):
            return (i + 1) & (SG - 1) if s[1] < AHEAD else i

        def qr_ready(j):
            return job["qr", j] - NJ if j < AHEAD else job["qr", j]

        assert NJ % NB == 0

        with nc.Block() as block:
            @block.sync
            def _(sp):
                sp.dma_start(cos[:, :, :], A["cos"]).then_inc(table_in, 16)
                sp.dma_start(sin[:, :, :], A["sin"]).then_inc(table_in, 16)
                kv_d = A["ctx"][:, 0:LC * P, :].rearrange("(g b) (c p) d -> g p b c d", b=BT, p=P)
                last_d = sh.last_dram.rearrange("(i o b) d -> i o b d", o=1, b=GB)
                def load_keys(i, k):
                    sp.wait_ge(raw_free, 3 * (2 * i + k + 1))
                    for b in range(BT):
                        sp.dma_start(raw[:, k, b], kv_d[2 * i + k, :, b]).then_inc(raw_in[k], 16)

                def store_tile(i, k):
                    sp.wait_ge(free, NB + NJ * i + job["av", 4 * k + 3] + 1)
                    sp.dma_start(sh.ctx_dram[2 * i + k], out[:, :, :].rearrange("p h t -> p (h t)")).then_inc(out_done, 16)

                def last_row(i):
                    sp.dma_start(last[:, :, :], last_d[i]).then_inc(last_in, 16)

                unfilled = sh.sorted_dram.rearrange("(i n p) d -> i p n d", i=SG, p=P)
                unused = sh.y_dram[MINTILE * E * P:].rearrange("(i n p) d -> i p n d", i=SG, p=P)
                sp.wait_ge(zero_done, 1)

                def fill(i):
                    for rows in (unfilled, unused):
                        sp.dma_start(rows[i], zero[:, :].unsqueeze(1).to_broadcast([P, rows.shape[2], D])).then_inc(zero_out, 16)

                load_keys(0, 0)
                load_keys(0, 1)
                last_row(0)
                with sp.Fori(0, SG - 1) as i:
                    load_keys(i + 1, 0)
                    load_keys(i + 1, 1)
                    fill(i)
                    store_tile(i, 0)
                    store_tile(i, 1)
                    last_row(i + 1)
                fill(SG - 1)
                store_tile(SG - 1, 0)
                store_tile(SG - 1, 1)
                sp.wait_ge(zero_out, 16 * 2 * SG)

            @block.gpsimd
            def _(pool):
                nc.gpsimd.memset(zero[:, :], 0.0).then_inc(zero_done, 1)
                nc.gpsimd.memset(kT_hi[:, :, :, L:LP].bitcast(F32), 0.0).then_inc(pad_done, 1)
                nc.gpsimd.memset(kT_lo[:, :, :, L:LP].bitcast(F32), 0.0).then_inc(pad_done, 1)
                pool.sem_inc(raw_free, 6)
                pool.wait_ge(table_in, 32)
                with pool.Fori(0, SG) as i:
                    for k in range(2):
                        pool.wait_ge(raw_in[k], 16 * BT * (i + 1))
                        if k == 1:
                            pool.wait_ge(ready, NJ * i + job["kT", 0, LC - 1] + 1)
                        v, o = raw[:, k].rearrange("p b c d -> p b (c d)"), rot[:, :].rearrange("p b c d -> p b (c d)")
                        cb = cos[:, :, :].rearrange("p c d -> p (c d)").unsqueeze(1).to_broadcast([P, BT, LC * DC])
                        nc.gpsimd.tensor_tensor(o, v, cb, ALU.mult).then_inc(raw_free, 1)
                        for a in range(2):
                            to, of = slice(64 * a, 64 * a + 64), slice(64 - 64 * a, 128 - 64 * a)
                            sb_ = sin[:, :, to].unsqueeze(1).to_broadcast([P, BT, LC, 64])
                            nc.gpsimd.tensor_tensor(half[:, :, :, to], raw[:, k, :, :, of], sb_, ALU.mult).then_inc(raw_free, 1)
                        pool.wait_ge(raw_free, 6 + 3 * (2 * i + k + 1))
                        nc.gpsimd.tensor_tensor(o, o, half[:, :].rearrange("p b c d -> p b (c d)"), ALU.add).then_inc(rot_done, 1)
                        pool.wait_ge(rot_done, 2 * i + k + 1)
                        pool.wait_ge(nat_hi, 2 * i + k + 1)
                        for kT, lT in ((kT_hi, sh.lastT_hi), (kT_lo, sh.lastT_lo)):
                            nc.gpsimd.tensor_copy(kT[:, k, :, L - 1:L],
                                                  lT[:, bass.ds(i * GB + k * BT, BT)].bitcast(F32).unsqueeze(2)).then_inc(kv_done, 1)
                        nc.gpsimd.tensor_tensor(kv_lo[:, k], rot[:, :], kv_hi[:, k].bitcast(F32), ALU.subtract).then_inc(kv_done, 1)
                        pool.wait_ge(kv_done, 3 * (2 * i + k + 1))
                    for b in range(GB):
                        pool.wait_ge(recip_done, GB * i + b + 1)
                        nc.gpsimd.tensor_tensor(attn[:, b % 3], attn[:, b % 3], recip[:, b % 3].unsqueeze(2).to_broadcast([P, 4, L]),
                                                ALU.mult).then_inc(norm_done, 1)

            @block.scalar
            def _(act):
                for j in range(AHEAD):
                    act.wait_ge(ready, j + 1)
                    nc.scalar.copy(qr_hi[:, j % NQ], ring[j][:, 0:GT]).then_inc(hi_done, 1)
                with act.Fori(0, SG) as i:
                    def hi_copy(s, dst, src):
                        act.wait_ge(ready, NJ * i + job[s] + 1)
                        nc.scalar.copy(dst, src).then_inc(hi_done, 1)

                    for s in steps:
                        bank = ring[job[s] % NB] if s in job else None
                        if s[0] == "qr":
                            hi_copy(s, qr_hi[:, s[1] % NQ], bank[:, 0:GT])
                        elif s[0] == "qp":
                            j = s[1]
                            hi_copy(s, qp_hi[:, :, 2 * j:2 * j + 2, :].rearrange("p b h s -> p h b s"),
                                    bank[:, :].rearrange("p (h b s) -> p h b s", h=2, b=GB))
                        elif s[0] == "kT":
                            _, k, c = s
                            hi_copy(s, kT_hi[:, k, :, c * P:(c + 1) * P], bank[:, :].rearrange("p (b l) -> p b l", b=BT))
                        elif s[0] == "kv":
                            act.wait_ge(rot_done, 2 * i + s[1] + 1)
                            nc.scalar.copy(kv_hi[:, s[1]], rot[:, :]).then_inc(nat_hi, 1)
                        elif s[0] == "aT" and s[2] < LC:
                            hi_copy(s, aT_hi[:, s[2]], bank[:, :])
                        elif s[0] == "sc":
                            b = s[1]
                            for g in range(4):
                                act.wait_ge(max_done, 4 * GB * i + 4 * b + g + 1)
                                nc.scalar.activation(attn[:, b % 3, g], score[g][:, 0:L], ACT.Exp, bias=negmax[:, b % 3, g:g + 1],
                                                     accum_out=total[:, b % 3, g:g + 1]).then_inc(exp_done, 1)

            @block.vector
            def _(dve):
                dve.sem_inc(free, NB)
                dve.sem_inc(out_done, 16)
                for j in range(AHEAD):
                    dve.wait_ge(hi_done, j + 1)
                    split_lo(nc, qr_lo[:, j % NQ], ring[j][:, 0:GT], qr_hi[:, j % NQ]).then_inc(free, 1)
                dve.wait_ge(free, NB + AHEAD)
                dve.sem_inc(free, 1)
                with dve.Fori(0, SG) as i:
                    for s in steps:
                        bank = ring[job[s] % NB] if s in job else None
                        if s in split:
                            dve.wait_ge(hi_done, NS * i + split[s] + 1)
                        elif s in job:
                            dve.wait_ge(ready, NJ * i + job[s] + 1)
                        if s[0] == "qr":
                            split_lo(nc, qr_lo[:, s[1] % NQ], bank[:, 0:GT], qr_hi[:, s[1] % NQ]).then_inc(free, 1)
                        elif s[0] == "qp":
                            at = slice(2 * s[1], 2 * s[1] + 2)
                            split_lo(nc, qp_lo[:, :, at, :].rearrange("p b h s -> p h b s"),
                                     bank[:, :].rearrange("p (h b s) -> p h b s", h=2, b=GB),
                                     qp_hi[:, :, at, :].rearrange("p b h s -> p h b s")).then_inc(free, 1)
                        elif s[0] == "kT":
                            _, k, c = s
                            at = slice(c * P, (c + 1) * P)
                            split_lo(nc, kT_lo[:, k, :, at], bank[:, :].rearrange("p (b l) -> p b l", b=BT), kT_hi[:, k, :, at]).then_inc(free, 1)
                        elif s[0] == "sc":
                            b = s[1]
                            for g in range(4):
                                dve.wait_ge(score_ready, 4 * GB * i + 4 * b + g + 1)
                                nc.vector.tensor_reduce(negmax[:, b % 3, g:g + 1], score[g][:, 0:L], AX, ALU.max, negate=True).then_inc(max_done, 1)
                        elif s[0] == "rc":
                            b = s[1]
                            dve.wait_ge(exp_done, 4 * GB * i + 4 * b + 4)
                            nc.vector.reciprocal(recip[:, b % 3], total[:, b % 3]).then_inc(recip_done, 1)
                        elif s[0] == "aT":
                            c = s[2]
                            if c < LC:
                                split_lo(nc, aT_lo[:, c], bank[:, :], aT_hi[:, c]).then_inc(free, 1)
                            else:
                                nc.vector.tensor_copy(aT_last[:, :], bank[0:1, :]).then_inc(free, 1)
                        elif s[0] == "av":
                            b = s[1]
                            if b % BT == 0:
                                dve.wait_ge(out_done, 16 * (2 * i + b // BT + 1))
                            nc.vector.tensor_copy(out[:, :, (b % BT) * S:(b % BT + 1) * S],
                                                  bank[:, :].rearrange("p (h s) -> p h s", h=H)).then_inc(free, 1)

            @block.tensor
            def _(pe):
                pe.wait_ge(pad_done, 2)

                def score_rank(bank, j, group):
                    w, at = slice(j * P, (j + 1) * P), bass.ds(group * GT, GT)
                    for c in range(DCH):
                        mm = three_passes(nc, bank[:, 0:GT], sh.m1_hi[:, c, w], sh.m1_lo[:, c, w],
                                          sh.xT_hi[:, c, at], sh.xT_lo[:, c, at], c == 0, c == DCH - 1)
                    mm.then_inc(ready, 1)

                for j in range(AHEAD):
                    pe.wait_ge(free, j + 1)
                    score_rank(ring[j], j, 0)
                pe.wait_ge(ready, AHEAD)
                pe.sem_inc(ready, 1)
                with pe.Fori(0, SG) as i:
                    for s in steps:
                        n = job.get(s)
                        if n is not None:
                            bank = ring[n % NB]
                            pe.wait_ge(free, NJ * i + n + 1)
                        if s[0] == "qr":
                            score_rank(bank, s[1], tokens_of(s, i))
                        elif s[0] == "qp":
                            j = s[1]
                            pe.wait_ge(free, NB + NJ * i + qr_ready(j) + 1)
                            for e in range(2):
                                mm = three_passes(nc, bank[:, e * GT:(e + 1) * GT], sh.krT_hi[:, 2 * j + e], sh.krT_lo[:, 2 * j + e],
                                                  qr_hi[:, j % NQ], qr_lo[:, j % NQ], True, True)
                            mm.then_inc(ready, 1)
                        elif s[0] == "kT":
                            _, k, c = s
                            pe.wait_ge(rot_done, 2 * i + k + 1)
                            for b in range(BT):
                                mm = nc.tensor.transpose(bank[:, b * P:(b + 1) * P], rot[:, b, c], sh.ident[:, :])
                            mm.then_inc(ready, 1)
                        elif s[0] == "sc":
                            b = s[1]
                            k = b // BT
                            if b % BT == 0:
                                pe.wait_ge(kv_done, 3 * (2 * i + k + 1))
                                pe.wait_ge(free, NB + NJ * i + (job["qp", PAIRS - 1] if k == 0 else job["kT", 1, LC - 1]) + 1)
                            for g in range(4):
                                lhs = [q[:, b, 4 * g:4 * g + 4, :].rearrange("p h s -> p (h s)") for q in (qp_hi, qp_lo)]
                                if b > 0:
                                    pe.wait_ge(exp_done, 4 * GB * i + 4 * (b - 1) + g + 1)
                                three_passes(nc, score[g][:, 0:LP], lhs[0], lhs[1], kT_hi[:, k, b % BT], kT_lo[:, k, b % BT],
                                             True, True).then_inc(score_ready, 1)
                        elif s[0] == "aT":
                            _, b, c = s
                            if c == LC:
                                pe.wait_ge(norm_done, GB * i + b + 1)
                            w = P if c < LC else 1
                            for g in range(4):
                                mm = nc.tensor.transpose(bank[0:w, g * P:(g + 1) * P], attn[:, b % 3, g, c * P:c * P + w], sh.ident[:, :])
                            mm.then_inc(ready, 1)
                        elif s[0] == "av":
                            b = s[1]
                            k = b // BT
                            if b == 0:
                                pe.wait_ge(last_in, 16 * (i + 1))
                            pe.wait_ge(free, NB + NJ * i + job["aT", b, LC] + 1)
                            nc.tensor.matmul(bank[:, :], last[0:1, b, :], aT_last[:, :], start=True, stop=False)
                            for c in range(LC):
                                pe.wait_ge(free, NB + NJ * i + job["aT", b, c] + 1)
                                mm = three_passes(nc, bank[:, :], kv_hi[:, k, b % BT, c], kv_lo[:, k, b % BT, c],
                                                  aT_hi[:, c], aT_lo[:, c], False, c == LC - 1)
                            mm.then_inc(ready, 1)


def project_context(nc, A, sh):
    with ExitStack() as ctx:
        def sb(name, shape, dt=F32):
            return ctx.enter_context(nc.sbuf_tensor("o_" + name, shape, dt))

        def sem(name):
            return ctx.enter_context(nc.semaphore("o_" + name))

        HG, NW = 4, 3
        wo = sb("wo", [P, DCH, H * P])
        kckv = sb("kckv", [P, H, DC])
        woT = sb("woT", [P, NW, D])
        wm_hi, wm_lo = sb("wm_hi", [P, H, D], F32R), sb("wm_lo", [P, H, D], F32R)
        raw = sb("raw", [P, 2, H, P])
        c_hi, c_lo = sb("c_hi", [P, 2, H, P], F32R), sb("c_lo", [P, 2, H, P], F32R)
        NB = 6
        ring = [ctx.enter_context(nc.psum_tensor(f"o_ring{n}", [P, BANK], F32)) for n in range(NB)]
        acc = [ctx.enter_context(nc.psum_tensor(f"o_acc{n}", [P, BANK], F32)) for n in range(2)]

        wo_in, kckv_in, x_in = [sem(f"wo_in{g}") for g in range(H // HG)], sem("kckv_in"), sem("x_in")
        raw_in = [sem("raw_in0"), sem("raw_in1")]
        ready, hi_done, free = sem("ready"), sem("hi"), sem("free")
        c_hi_done, c_lo_done, acc_ready, acc_free = sem("c_hi_done"), sem("c_lo_done"), sem("acc_ready"), sem("acc_free")

        steps = [("woT", 0), ("woT", 1)]
        for h in range(H):
            steps += ([("woT", h + 2)] if h + 2 < H else []) + [("wm", h)]
        job = {s: n for n, s in enumerate(steps)}
        split = numbered(steps, ("wm",))
        C_SPLIT = ("wm", H - 6)

        with nc.Block() as block:
            @block.sync
            def _(sp):
                wo_d = A["Wo"].rearrange("(c o) n -> o c n", o=P)
                for g in range(H // HG):
                    at = slice(g * HG * P, (g + 1) * HG * P)
                    sp.dma_start(wo[:, :, at], wo_d[:, :, at]).then_inc(wo_in[g], 16)
                    if g == 0:
                        sp.dma_start(kckv[:, :, :], A["w_kc_kv"].rearrange("h k c -> k h c")).then_inc(kckv_in, 16)
                sp.wait_ge(sh.ctx_stored, 16 * (NT + 1))
                with sp.Fori(0, NT // 2) as i:
                    for k in range(2):
                        sp.wait_ge(c_lo_done, 2 * i + k + 1)
                        sp.dma_start(raw[:, k].rearrange("p h t -> p (h t)"), sh.ctx_dram[2 * i + k]).then_inc(raw_in[k], 16)

            @block.gpsimd
            def _(pool):
                pool.wait_ge(c_hi_done, 1)
                nc.gpsimd.tensor_tensor(c_lo[:, 0], raw[:, 0], c_hi[:, 0].bitcast(F32), ALU.subtract).then_inc(c_lo_done, 1)

            @block.scalar
            def _(act):
                def c_copy(k, i):
                    act.wait_ge(raw_in[k], 16 * (i + 1))
                    act.wait_ge(acc_ready, 2 * i + k + 1)
                    nc.scalar.copy(c_hi[:, k], raw[:, k]).then_inc(c_hi_done, 1)

                for s in steps:
                    if s[0] == "wm":
                        act.wait_ge(ready, job[s] + 1)
                        nc.scalar.copy(wm_hi[:, s[1]], ring[job[s] % NB][:, :]).then_inc(hi_done, 1)
                    if s == ("wm", H // 2):
                        act.dma_start(sh.x[:, :, :], A["x"].rearrange("b s d -> (b s) d").rearrange("(n p) d -> p n d", p=P)).then_inc(x_in, 16)
                    if s == C_SPLIT:
                        c_copy(0, 0)
                with act.Fori(0, NT // 2 - 1) as i:
                    c_copy(1, i)
                    c_copy(0, i + 1)
                c_copy(1, NT // 2 - 1)

            @block.vector
            def _(dve):
                dve.sem_inc(c_lo_done, 2)
                dve.sem_inc(acc_free, 2)
                def c_split(k, hi_count):
                    dve.wait_ge(c_hi_done, hi_count)
                    nc.vector.tensor_tensor(c_lo[:, k], raw[:, k], c_hi[:, k].bitcast(F32), ALU.subtract).then_inc(c_lo_done, 1)

                def add(k, t):
                    dve.wait_ge(acc_ready, 2 + t + 1)
                    at = sh.x[:, bass.ds(t, 1), :].rearrange("p n d -> p (n d)")
                    nc.vector.tensor_tensor(at, acc[k][:, :], at, ALU.add).then_inc(acc_free, 1)
                    dve.wait_ge(acc_free, 2 + t + 1)
                    sh.self_norm.statistics(at, t)

                for s in steps:
                    bank = ring[job[s] % NB]
                    if s[0] == "wm":
                        dve.wait_ge(hi_done, split[s] + 1)
                        split_lo(nc, wm_lo[:, s[1]], bank[:, :], wm_hi[:, s[1]]).then_inc(free, 1)
                    else:
                        dve.wait_ge(ready, job[s] + 1)
                        nc.vector.tensor_copy(woT[:, s[1] % NW], bank[:, :]).then_inc(free, 1)
                dve.wait_ge(x_in, 16)
                dve.wait_ge(c_lo_done, 2 + 1)
                with dve.Fori(0, NT // 2 - 1) as i:
                    for k in range(2):
                        c_split(1 - k, 2 * i + k + 2)
                        add(k, 2 * i + k)
                c_split(1, NT)
                for k in range(2):
                    add(k, NT - 2 + k)

            @block.tensor
            def _(pe):
                pe.sem_inc(acc_ready, 2)
                for s in steps:
                    n, h = job[s], s[1]
                    bank = ring[n % NB]
                    if n >= NB:
                        pe.wait_ge(free, n - NB + 1)
                    if s[0] == "woT":
                        if h % HG == 0:
                            pe.wait_ge(wo_in[h // HG], 16)
                        for c in range(DCH):
                            mm = nc.tensor.transpose(bank[:, c * P:(c + 1) * P], wo[:, c, h * P:(h + 1) * P], sh.ident[:, :])
                    else:
                        pe.wait_ge(kckv_in, 16)
                        pe.wait_ge(free, job["woT", h] + 1)
                        mm = nc.tensor.matmul(bank[:, :], kckv[:, h], woT[:, h % NW], start=True, stop=True)
                    mm.then_inc(ready, 1)
                pe.wait_ge(free, len(steps))
                with pe.Fori(0, NT // 2) as i:
                    for k in range(2):
                        pe.wait_ge(c_lo_done, 2 + 2 * i + k + 1)
                        pe.wait_ge(acc_free, 2 * i + k + 1)
                        for h in range(H):
                            mm = three_passes(nc, acc[k][:, :], c_hi[:, k, h], c_lo[:, k, h], wm_hi[:, h], wm_lo[:, h], h == 0, h == H - 1)
                        mm.then_inc(acc_ready, 1)


def self_attention(nc, A, sh):
    with ExitStack() as ctx:
        def sb(name, shape, dt=F32):
            return ctx.enter_context(nc.sbuf_tensor("s_" + name, shape, dt))

        def sem(name):
            return ctx.enter_context(nc.semaphore("s_" + name))

        SCALE = float(1.0 / np.sqrt(P))
        HALVES = T // BANK
        BH = B // HALVES
        xn = sb("xn", [P, 2, D])
        xT_hi, xT_lo = sb("xT_hi", [P, DCH, T], F32R), sb("xT_lo", [P, DCH, T], F32R)
        wq, wk, wo = sb("wq", [P, G, D]), sb("wk", [P, D]), sb("wo", [P, DCH, G * P])
        wqT_hi, wqT_lo = sb("wqT_hi", [P, DCH, G * P], F32R), sb("wqT_lo", [P, DCH, G * P], F32R)
        wkT_hi, wkT_lo = sb("wkT_hi", [P, DCH, P], F32R), sb("wkT_lo", [P, DCH, P], F32R)
        woT_hi, woT_lo = sb("woT_hi", [P, G, D], F32R), sb("woT_lo", [P, G, D], F32R)
        kT = sb("kT", [P, T])
        qT = sb("qT", [P, B, G, S])
        v_all = sb("v_all", [P, NT, KVH * P])
        v = sb("v", [P, NT, P])
        mask = sb("mask", [P, S])
        prob = sb("prob", [P, HALVES, BH, S])
        peak, total, recip = (sb(n, [P, HALVES, BH]) for n in ("peak", "total", "recip"))
        pT = sb("pT", [P, HALVES, BANK])
        o_hi, o_lo = sb("o_hi", [P, G, T], F32R), sb("o_lo", [P, G, T], F32R)
        wv = qT[:, :, :, :].rearrange("p b g s -> p (b g s)")[:, 0:KVH * D].rearrange("p (c d) -> p c d", c=KVH)
        wvT_hi = o_hi[:, 0:2, :].rearrange("p g t -> p (g t)").rearrange("p (c n) -> p c n", c=DCH)
        wvT_lo = o_lo[:, 0:2, :].rearrange("p g t -> p (g t)").rearrange("p (c n) -> p c n", c=DCH)
        ln = sh.self_norm
        NB = 4
        ring = [ctx.enter_context(nc.psum_tensor(f"s_ring{n}", [P, BANK], F32)) for n in range(NB)]
        score = [ctx.enter_context(nc.psum_tensor(f"s_score{n}", [P, BANK], F32)) for n in range(HALVES)]

        wq_in, wk_in, wo_in, wv_in, mask_in = (sem(n) for n in ("wq_in", "wk_in", "wo_in", "wv_in", "mask_in"))
        xn_done, v_done = sem("xn_done"), sem("v_done")
        pready, phi, pfree = sem("pready"), sem("phi"), sem("pfree")
        ready, hi_done, free = sem("ready"), sem("hi"), sem("free")
        score_ready, prob_done, shifted, exp_done, soft = (sem(n) for n in ("score_ready", "prob_done", "shifted", "exp_done", "soft"))

        qk_weights = [("wkT", c) for c in range(DCH)] + [("wqT", c) for c in range(DCH)]
        first = [("xT", 0), ("xT", 1)] + [("wvT", c) for c in range(DCH)] + [("xT", t) for t in range(2, NT)]
        first += qk_weights + [("v", t) for t in range(NT)]
        fjob, fsplit = numbered(first, ("wvT", "xT", "wkT", "wqT", "v")), numbered(first, ("wvT", "xT", "wkT", "wqT"))

        steps = [("kT", a) for a in range(HALVES)] + [("qT", g, 0) for g in range(G)]
        steps += [("qT", 0, 1), ("half_sc", 0), ("qT", 1, 1), ("sc", 0), ("mx", 0), ("qT", 2, 1), ("nm", 0), ("qT", 3, 1)]
        steps += [("woT", 0), ("woT", 1), ("half_sc", 1), ("pT", 0), ("woT", 2), ("woT", 3)] + [("oT", 0, b) for b in range(BT)]
        steps_to_oT = steps
        steps = steps_to_oT + qk_weights[:-2] + [("out", 0), ("sc", 1), ("mx", 1), ("out", 1), ("nm", 1), ("out", 2), ("pT", 1)]
        steps += qk_weights[-2:] + [("oT", 1, b) for b in range(BT)] + [("out", t) for t in range(NT // 2 - 1, NT)]

        def numbers(steps):
            return steps, numbered(steps, ("wkT", "wqT", "woT", "kT", "qT", "pT", "oT", "out")), numbered(steps, ("wkT", "wqT", "woT", "oT"))

        usual = numbers(steps)
        final = numbers(steps_to_oT + [("sc", 1), ("mx", 1), ("out", 0), ("nm", 1), ("out", 1), ("pT", 1), ("out", 2)]
                        + [("oT", 1, b) for b in range(BT)] + [("out", t) for t in range(NT // 2 - 1, NT)])
        _, job, split = usual
        NJ, NS = len(job), len(split)
        assert NJ % NB == 0 and job["wqT", DCH - 1] + NB < NJ and job["woT", G - 1] < job["oT", 0, 0]
        SOFT = 5

        def o_at(o, a, b):
            return o[:, :, a * BANK:(a + 1) * BANK].rearrange("p g (n b t) -> p n b g t", n=BH // BT, b=BT)[:, :, b]

        with nc.Block() as block:
            @block.sync
            def _(sp):
                sp.dma_start(wv, A["wv"].rearrange("(c k) d -> k c d", k=P)).then_inc(wv_in, 16)
                wq_d = A["wq"].rearrange("(j g k) d -> j k g d", g=G, k=P)
                wk_d = A["wk"].rearrange("(j k) d -> j k d", k=P)
                wo_d = A["wo"].rearrange("(c o) (j n) -> j o c n", o=P, j=KVH)
                sp.dma_start(wk[:, :], wk_d[0]).then_inc(wk_in, 16)
                sp.dma_start(wq[:, :, :], wq_d[0]).then_inc(wq_in, 16)
                sp.dma_start(mask[:, :], A["mask"]).then_inc(mask_in, 16)
                sp.wait_ge(pready, fjob["wqT", DCH - 1] + 1)
                with sp.Fori(0, KVH - 1) as i:
                    sp.wait_ge(ready, NJ * i + job["wqT", DCH - 1] + 1)
                    sp.dma_start(wo[:, :, :], wo_d[i]).then_inc(wo_in, 16)
                    sp.dma_start(wk[:, :], wk_d[i + 1]).then_inc(wk_in, 16)
                    sp.dma_start(wq[:, :, :], wq_d[i + 1]).then_inc(wq_in, 16)
                sp.wait_ge(ready, NJ * (KVH - 1) + job["wqT", DCH - 1] + 1)
                sp.dma_start(wo[:, :, :], wo_d[KVH - 1]).then_inc(wo_in, 16)

            @block.gpsimd
            def _(pool):
                with pool.Fori(0, KVH) as i:
                    pool.wait_ge(pfree, len(first) + NB)
                    pool.wait_ge(ready, NJ + NJ * i + job["kT", 0] + 1)
                    nc.gpsimd.tensor_copy(v[:, :, :], v_all[:, :, bass.ds(i * P, P)]).then_inc(v_done, 1)

            @block.scalar
            def _(act):
                ln.take_root(act, 0, NT)
                for s in first:
                    bank = ring[fjob[s] % NB]
                    if s in fsplit:
                        act.wait_ge(pready, fjob[s] + 1)
                        if s[0] == "wvT":
                            nc.scalar.copy(wvT_hi[:, s[1]], bank[:, :]).then_inc(phi, 1)
                        elif s[0] == "wkT":
                            nc.scalar.copy(wkT_hi[:, s[1]], bank[:, 0:P]).then_inc(phi, 1)
                        elif s[0] == "wqT":
                            nc.scalar.copy(wqT_hi[:, s[1]], bank[:, :]).then_inc(phi, 1)
                        else:
                            nc.scalar.copy(xT_hi[:, :, s[1] * P:(s[1] + 1) * P], bank[:, :].rearrange("p (c t) -> p c t", c=DCH)).then_inc(phi, 1)
                def head(i, steps, job, split, last):
                    for s in steps:
                        if s in split:
                            bank = ring[job[s] % NB]
                            act.wait_ge(ready, NJ + NJ * i + job[s] + 1)
                        if s[0] == "wkT":
                            nc.scalar.copy(wkT_hi[:, s[1]], bank[:, 0:P]).then_inc(hi_done, 1)
                        elif s[0] == "wqT":
                            nc.scalar.copy(wqT_hi[:, s[1]], bank[:, :]).then_inc(hi_done, 1)
                        elif s[0] == "woT":
                            nc.scalar.copy(woT_hi[:, s[1]], bank[:, :]).then_inc(hi_done, 1)
                        elif s[0] == "oT":
                            nc.scalar.copy(o_at(o_hi, s[1], s[2]), bank[:, :].rearrange("p (n g t) -> p n g t", n=BH // BT, g=G)).then_inc(hi_done, 1)
                        elif s[0] == "mx":
                            a = s[1]
                            act.wait_ge(shifted, HALVES * i + a + 1)
                            nc.scalar.activation(prob[:, a], prob[:, a], ACT.Exp).then_inc(exp_done, 1)

                with act.Fori(0, KVH - 1) as i:
                    head(i, *usual, False)
                head(KVH - 1, *final, True)

            @block.vector
            def _(dve):
                ln.variance(dve, 0, NT)
                ln.power(dve, 0, NT)

                def norm(t):
                    if t >= 2:
                        dve.wait_ge(pready, fjob["xT", t - 2] + 1)
                    ln.apply(t, xn[:, t % 2], sh.x[:, t]).then_inc(xn_done, 1)

                norm(0)
                norm(1)
                dve.sem_inc(pfree, NB)
                for s in first:
                    bank = ring[fjob[s] % NB]
                    if s in fsplit:
                        dve.wait_ge(phi, fsplit[s] + 1)
                    else:
                        dve.wait_ge(pready, fjob[s] + 1)
                    if s[0] == "wvT":
                        split_lo(nc, wvT_lo[:, s[1]], bank[:, :], wvT_hi[:, s[1]]).then_inc(pfree, 1)
                    elif s[0] == "xT":
                        at = slice(s[1] * P, (s[1] + 1) * P)
                        split_lo(nc, xT_lo[:, :, at], bank[:, :].rearrange("p (c t) -> p c t", c=DCH), xT_hi[:, :, at]).then_inc(pfree, 1)
                        if s[1] + 2 < NT:
                            norm(s[1] + 2)
                    elif s[0] == "wkT":
                        split_lo(nc, wkT_lo[:, s[1]], bank[:, 0:P], wkT_hi[:, s[1]]).then_inc(pfree, 1)
                    elif s[0] == "wqT":
                        split_lo(nc, wqT_lo[:, s[1]], bank[:, :], wqT_hi[:, s[1]]).then_inc(pfree, 1)
                    else:
                        nc.vector.tensor_copy(v_all[:, s[1]], bank[:, :]).then_inc(pfree, 1)
                dve.wait_ge(mask_in, 16)
                dve.sem_inc(free, NB + NJ)
                def head(i, steps, job, split, last):
                    def chained(instruction, a, n):
                        instruction.then_inc(soft, 1)
                        dve.wait_ge(soft, SOFT * (HALVES * i + a) + n)

                    for s in steps:
                        bank = ring[job[s] % NB] if s in job else None
                        if s in split:
                            dve.wait_ge(hi_done, NS * i + split[s] + 1)
                        elif s in job:
                            dve.wait_ge(ready, NJ + NJ * i + job[s] + 1)
                        if s[0] == "wkT":
                            split_lo(nc, wkT_lo[:, s[1]], bank[:, 0:P], wkT_hi[:, s[1]]).then_inc(free, 1)
                        elif s[0] == "wqT":
                            split_lo(nc, wqT_lo[:, s[1]], bank[:, :], wqT_hi[:, s[1]]).then_inc(free, 1)
                        elif s[0] == "woT":
                            split_lo(nc, woT_lo[:, s[1]], bank[:, :], woT_hi[:, s[1]]).then_inc(free, 1)
                        elif s[0] == "kT":
                            nc.vector.tensor_copy(kT[:, s[1] * BANK:(s[1] + 1) * BANK], bank[:, :]).then_inc(free, 1)
                        elif s[0] == "qT":
                            _, g, a = s
                            nc.vector.tensor_copy(qT[:, a * BH:(a + 1) * BH, g, :], bank[:, :].rearrange("p (b t) -> p b t", b=BH)).then_inc(free, 1)
                        elif s[0] == "mx":
                            a = s[1]
                            dve.wait_ge(score_ready, HALVES * i + a + 1)
                            chained(nc.vector.scalar_tensor_tensor(
                                prob[:, a], score[a][:, :].rearrange("p (b s) -> p b s", b=BH), SCALE,
                                mask[:, :].unsqueeze(1).to_broadcast([P, BH, S]), ALU.mult, ALU.add), a, 1)
                            chained(nc.vector.tensor_reduce(peak[:, a], prob[:, a], AX, ALU.max), a, 2)
                            nc.vector.tensor_tensor(prob[:, a], prob[:, a], peak[:, a].unsqueeze(2).to_broadcast([P, BH, S]),
                                                    ALU.subtract).then_inc(shifted, 1)
                        elif s[0] == "pT":
                            nc.vector.tensor_copy(pT[:, s[1]], bank[:, :]).then_inc(free, 1)
                        elif s[0] == "oT":
                            split_lo(nc, o_at(o_lo, s[1], s[2]), bank[:, :].rearrange("p (n g t) -> p n g t", n=BH // BT, g=G),
                                     o_at(o_hi, s[1], s[2])).then_inc(free, 1)
                        elif s[0] == "out":
                            nc.vector.tensor_tensor(sh.x[:, s[1]], bank[:, :], sh.x[:, s[1]], ALU.add).then_inc(free, 1)
                            if last:
                                dve.wait_ge(free, NB + NJ + NJ * i + job[s] + 1)
                                sh.route_norm.statistics(sh.x[:, s[1]], s[1])
                        elif s[0] == "nm":
                            a = s[1]
                            dve.wait_ge(exp_done, HALVES * i + a + 1)
                            chained(nc.vector.tensor_reduce(total[:, a], prob[:, a], AX, ALU.add), a, 3)
                            chained(nc.vector.tensor_scalar_max(total[:, a], total[:, a], 1e-9), a, 4)
                            chained(nc.vector.reciprocal(recip[:, a], total[:, a]), a, 5)
                            nc.vector.tensor_tensor(prob[:, a], prob[:, a], recip[:, a].unsqueeze(2).to_broadcast([P, BH, S]),
                                                    ALU.mult).then_inc(prob_done, 1)

                with dve.Fori(0, KVH - 1) as i:
                    head(i, *usual, False)
                head(KVH - 1, *final, True)

            @block.tensor
            def _(pe):
                def transpose_wk(bank, c, i):
                    if c == 0:
                        pe.wait_ge(wk_in, 16 * (i + 1))
                    return nc.tensor.transpose(bank[:, 0:P], wk[:, c * P:(c + 1) * P], sh.ident[:, :])

                def transpose_wq(bank, c, i):
                    if c == 0:
                        pe.wait_ge(wq_in, 16 * (i + 1))
                    for g in range(G):
                        mm = nc.tensor.transpose(bank[:, g * P:(g + 1) * P], wq[:, g, c * P:(c + 1) * P], sh.ident[:, :])
                    return mm

                pe.sem_inc(ready, NJ)
                for s in first:
                    n = fjob[s]
                    bank = ring[n % NB]
                    pe.wait_ge(pfree, n + 1)
                    if s[0] == "wvT":
                        pe.wait_ge(wv_in, 16)
                        for j in range(KVH):
                            mm = nc.tensor.transpose(bank[:, j * P:(j + 1) * P], wv[:, j, s[1] * P:(s[1] + 1) * P], sh.ident[:, :])
                    elif s[0] == "xT":
                        pe.wait_ge(xn_done, s[1] + 1)
                        for c in range(DCH):
                            mm = nc.tensor.transpose(bank[:, c * P:(c + 1) * P], xn[:, s[1] % 2, c * P:(c + 1) * P], sh.ident[:, :])
                    elif s[0] == "wkT":
                        mm = transpose_wk(bank, s[1], 0)
                    elif s[0] == "wqT":
                        mm = transpose_wq(bank, s[1], 0)
                    else:
                        pe.wait_ge(pfree, NB + fjob["xT", NT - 1] + 1)
                        at = slice(s[1] * P, (s[1] + 1) * P)
                        for c in range(DCH):
                            mm = three_passes(nc, bank[:, :], xT_hi[:, c, at], xT_lo[:, c, at], wvT_hi[:, c], wvT_lo[:, c], c == 0, c == DCH - 1)
                    mm.then_inc(pready, 1)
                pe.wait_ge(pfree, NB + len(first))
                def head(i, steps, job, split, last):
                    for s in steps:
                        source = {"half_sc": ("qT", G - 1, s[1]), "oT": ("pT", s[1]), "out": ("oT", s[1] // (NT // 2), BT - 1)}.get(s[0])
                        settled = [NB + job[source]] if source else []
                        emptied = [job[s]] if s in job else []
                        if s in job:
                            bank = ring[job[s] % NB]
                        if settled or emptied:
                            pe.wait_ge(free, NJ + NJ * i + max(settled + emptied) + 1)
                        if s[0] == "wkT":
                            mm = transpose_wk(bank, s[1], i + 1)
                        elif s[0] == "wqT":
                            mm = transpose_wq(bank, s[1], i + 1)
                        elif s[0] == "woT":
                            if s[1] == 0:
                                pe.wait_ge(wo_in, 16 * (i + 1))
                            for c in range(DCH):
                                mm = nc.tensor.transpose(bank[:, c * P:(c + 1) * P], wo[:, c, s[1] * P:(s[1] + 1) * P], sh.ident[:, :])
                        elif s[0] == "kT":
                            at = slice(s[1] * BANK, (s[1] + 1) * BANK)
                            for c in range(DCH):
                                mm = three_passes(nc, bank[:, :], wkT_hi[:, c], wkT_lo[:, c], xT_hi[:, c, at], xT_lo[:, c, at], c == 0, c == DCH - 1)
                        elif s[0] == "qT":
                            _, g, a = s
                            at, w = slice(a * BANK, (a + 1) * BANK), slice(g * P, (g + 1) * P)
                            for c in range(DCH):
                                mm = three_passes(nc, bank[:, :], wqT_hi[:, c, w], wqT_lo[:, c, w], xT_hi[:, c, at], xT_lo[:, c, at], c == 0, c == DCH - 1)
                        elif s[0] in ("half_sc", "sc"):
                            a = s[1]
                            for n in (range(BH // 2) if s[0] == "half_sc" else range(BH // 2, BH)):
                                b = a * BH + n
                                mm = nc.tensor.matmul(score[a][:, n * S:(n + 1) * S], qT[:, b].rearrange("p g s -> p (g s)"), kT[:, b * S:(b + 1) * S],
                                                      start=True, stop=True)
                            if s[0] == "sc":
                                mm.then_inc(score_ready, 1)
                        elif s[0] == "pT":
                            a = s[1]
                            pe.wait_ge(prob_done, HALVES * i + a + 1)
                            for n in range(BH // BT):
                                mm = nc.tensor.transpose(bank[:, n * P:(n + 1) * P], prob[:, a, n * BT:(n + 1) * BT, :].rearrange("p b s -> p (b s)"), sh.ident[:, :])
                        elif s[0] == "oT":
                            _, a, b = s
                            pe.wait_ge(v_done, i + 1)
                            rows = slice(b * S, (b + 1) * S)
                            for n in range(BH // BT):
                                mm = nc.tensor.matmul(bank[:, n * P:(n + 1) * P], v[rows, a * BH // BT + n], pT[rows, a, n * P:(n + 1) * P],
                                                      start=True, stop=True)
                        elif s[0] == "out":
                            t = s[1]
                            at = slice(t * P, (t + 1) * P)
                            for g in range(G):
                                mm = three_passes(nc, bank[:, :], o_hi[:, g, at], o_lo[:, g, at], woT_hi[:, g], woT_lo[:, g], g == 0, g == G - 1)
                        if s in job:
                            mm.then_inc(ready, 1)

                with pe.Fori(0, KVH - 1) as i:
                    head(i, *usual, False)
                head(KVH - 1, *final, True)


class ExpertWeights:
    HALF = M // 2
    UP, DOWN = 4, 2
    PIECES = UP + DOWN
    BY_VECTOR = PIECES - 1

    def __init__(self, nc, ctx, A):
        self.nc = nc
        self.raw = ctx.enter_context(nc.sbuf_tensor("w_raw", [P, self.PIECES, DCH * self.HALF], F32))
        self.hi, self.lo = (ctx.enter_context(nc.sbuf_tensor(f"w_{n}", [P, self.PIECES, DCH * self.HALF], F32R)) for n in ("hi", "lo"))
        self.raw_in = [ctx.enter_context(nc.semaphore(f"w_raw_in{p}")) for p in range(self.PIECES)]
        self.hi_ready, self.most_ready, self.last_ready = (
            ctx.enter_context(nc.semaphore(f"w_{n}")) for n in ("hi_ready", "most_ready", "last_ready"))
        self.up = [A[w].rearrange("e (c p) (u m) -> e u p c m", p=P, u=2) for w in ("w0", "w1")]
        self.down = A["ffn_wo"].rearrange("e (u q p) d -> e u p q d", p=P, u=2)

    def load(self, sp, e, p):
        src = self.up[p % 2][e, p // 2] if p < self.UP else self.down[e, p - self.UP]
        sp.dma_start(self.raw[:, p].rearrange("p (c m) -> p c m", c=DCH), src).then_inc(self.raw_in[p], 16)

    def wait_split(self, eng, e, p):
        if p < self.BY_VECTOR:
            eng.wait_ge(self.most_ready, self.BY_VECTOR * e + p + 1)
        else:
            eng.wait_ge(self.last_ready, e + 1)

    def write_hi(self, act, e, p):
        act.wait_ge(self.raw_in[p], 16 * (e + 1))
        self.nc.scalar.copy(self.hi[:, p], self.raw[:, p]).then_inc(self.hi_ready, 1)

    def write_lo(self, eng, to, e, p):
        done = self.most_ready if p < self.BY_VECTOR else self.last_ready
        eng.wait_ge(self.hi_ready, self.PIECES * e + p + 1)
        to.tensor_tensor(self.lo[:, p], self.raw[:, p], self.hi[:, p].bitcast(F32), ALU.subtract).then_inc(done, 1)


def route(nc, A, sh):
    with ExitStack() as ctx:
        def sb(name, shape, dt=F32):
            return ctx.enter_context(nc.sbuf_tensor("r_" + name, shape, dt))

        def sem(name):
            return ctx.enter_context(nc.semaphore("r_" + name))

        xn = sb("xn", [P, NT, D])
        xT = sb("xT", [P, DCH, BANK])
        logitT = sb("logitT", [E, T])
        gate = sb("gate", [P, DCH, E])
        before, ones = sb("before", [P, P]), sb("ones", [P, P])
        order, count_up = sb("order", [P, E]), sb("count_up", [P, T // P])
        logit, pick, first, second, both = (sb(n, [P, NT, E]) for n in ("logit", "pick", "first", "second", "both"))
        rank, scan, scan2, place = (sb(n, [P, NT, E]) for n in ("rank", "scan", "scan2", "place"))
        best, top1, top2, ratio, den = (sb(n, [P, NT]) for n in ("best", "top1", "top2", "ratio", "den"))
        pos = sb("pos", [P, 2, NT])
        tiles, start, start2 = (sb(n, [P, E]) for n in ("tiles", "start", "start2"))
        more = sb("more", [P, E, T // P - MINTILE])
        w = sh.weights
        ln = sh.route_norm
        HT = BANK // P
        tr = [ctx.enter_context(nc.psum_tensor(f"r_tr{n}", [P, BANK], F32)) for n in range(HT)]
        lgT = ctx.enter_context(nc.psum_tensor("r_lgT", [P, BANK], F32))
        lg = ctx.enter_context(nc.psum_tensor("r_lg", [P, BANK], F32))
        rk = ctx.enter_context(nc.psum_tensor("r_rk", [P, BANK], F32))
        tt = ctx.enter_context(nc.psum_tensor("r_tt", [P, BANK], F32))

        const_in, ones_done, xn_done, ready, free = sem("const_in"), sem("ones_done"), sem("xn_done"), sem("ready"), sem("free")
        half_ready, half_out = sem("half_ready"), sem("half_out")
        logits_ready, both_done, ranks_ready, gap_done, ratio_done = (
            sem(n) for n in ("logits_ready", "both_done", "ranks_ready", "gap_done", "ratio_done"))
        chain, pos_done, scattered = sem("chain"), sem("pos_done"), sem("scattered")

        with nc.Block() as block:
            @block.sync
            def _(sp):
                sp.dma_start(gate[:, :, :], A["gate_w"].rearrange("(c p) e -> p c e", p=P)).then_inc(const_in, 16)
                sp.dma_start(before[:, :], A["before"]).then_inc(const_in, 16)
                sp.dma_start(order[:, :], A["order"]).then_inc(const_in, 16)
                sp.dma_start(count_up[:, :], A["count_up"]).then_inc(const_in, 16)
                for p in range(w.PIECES):
                    w.load(sp, 0, p)

            @block.gpsimd
            def _(pool):
                nc.gpsimd.memset(ones[:, :], 1.0).then_inc(ones_done, 1)
                pool.wait_ge(pos_done, 1)
                rows = sh.sorted_dram
                for t in range(NT):
                    for k in range(2):
                        pool.indirect_dma_start(rows, bass.IndirectOffsetOnAxis(ap=sh.pos[:, k, t:t + 1], axis=0), xn[:, t], None).then_inc(scattered, 16)
                pool.wait_ge(scattered, 16 * 2 * NT)

            @block.scalar
            def _(act):
                ln.take_root(act, 0, NT)
                for t in range(NT):
                    act.wait_ge(ready, t + 1)
                    if t >= HT:
                        act.wait_ge(half_ready, t // HT)
                    at = slice(t % HT * P, (t % HT + 1) * P)
                    nc.scalar.copy(xT[:, :, at], tr[t % HT][:, :].rearrange("p (c t) -> p c t", c=DCH)).then_inc(free, 1)
                act.wait_ge(gap_done, 1)
                nc.scalar.activation(ratio[:, :], top2[:, :], ACT.Exp).then_inc(ratio_done, 1)
                for p in range(w.PIECES):
                    w.write_hi(act, 0, p)

            @block.tensor
            def _(pe):
                def token_tiles(a):
                    pe.wait_ge(half_out, a + 1)
                    for t in range(a * HT, (a + 1) * HT):
                        mm = nc.tensor.transpose(lg[:, t * E:(t + 1) * E], logitT[:, t * P:(t + 1) * P], sh.ident[0:E, 0:E])
                    return mm

                pe.wait_ge(const_in, 64)
                for a in range(NT // HT):
                    for t in range(a * HT, (a + 1) * HT):
                        pe.wait_ge(xn_done, t + 1)
                        if t >= HT:
                            pe.wait_ge(free, t - HT + 1)
                        for c in range(DCH):
                            mm = nc.tensor.transpose(tr[t % HT][:, c * P:(c + 1) * P], xn[:, t, c * P:(c + 1) * P], sh.ident[:, :])
                        mm.then_inc(ready, 1)
                    if a:
                        token_tiles(a - 1)
                    pe.wait_ge(free, (a + 1) * HT)
                    for c in range(DCH):
                        mm = nc.tensor.matmul(lgT[0:E, :], gate[:, c], xT[:, c], start=c == 0, stop=c == DCH - 1)
                    mm.then_inc(half_ready, 1)
                token_tiles(NT // HT - 1).then_inc(logits_ready, 1)
                pe.wait_ge(both_done, 1)
                pe.wait_ge(ones_done, 1)
                flat = both[:, :, :].rearrange("p t e -> p (t e)")
                nc.tensor.matmul(rk[:, 0:NT * E], before[:, :], flat, start=True, stop=True)
                nc.tensor.matmul(tt[:, 0:NT * E], ones[:, :], flat, start=True, stop=True).then_inc(ranks_ready, 1)

            @block.vector
            def _(dve):
                v = nc.vector
                ln.variance(dve, 0, NT)
                ln.power(dve, 0, NT)
                for t in range(NT):
                    ln.apply(t, xn[:, t], sh.x[:, t]).then_inc(xn_done, 1)
                for a in range(NT // HT):
                    dve.wait_ge(half_ready, a + 1)
                    v.tensor_copy(logitT[:, a * BANK:(a + 1) * BANK], lgT[0:E, :]).then_inc(half_out, 1)
                count = [0]

                def then(instruction):
                    instruction.then_inc(chain, 1)
                    count[0] += 1
                    dve.wait_ge(chain, count[0])

                def over_e(a):
                    return a.unsqueeze(2).to_broadcast([P, NT, E])

                order_b = order[:, :].unsqueeze(1).to_broadcast([P, NT, E])

                def choose(one_hot, top):
                    then(v.tensor_reduce(top[:, :], logit[:, :, :], AX, ALU.max))
                    then(v.tensor_tensor(pick[:, :, :], logit[:, :, :], over_e(top[:, :]), ALU.is_equal))
                    then(v.tensor_tensor(pick[:, :, :], pick[:, :, :], order_b, ALU.mult))
                    then(v.tensor_reduce(best[:, :], pick[:, :, :], AX, ALU.max))
                    then(v.tensor_tensor(one_hot[:, :, :], pick[:, :, :], over_e(best[:, :]), ALU.is_equal))

                dve.wait_ge(const_in, 64)
                dve.wait_ge(logits_ready, 1)
                then(v.tensor_copy(logit[:, :, :].rearrange("p t e -> p (t e)"), lg[:, 0:NT * E]))
                choose(first, top1)
                then(v.scalar_tensor_tensor(logit[:, :, :].rearrange("p t e -> p (t e)"), first[:, :, :].rearrange("p t e -> p (t e)"), MASKED,
                                            logit[:, :, :].rearrange("p t e -> p (t e)"), ALU.mult, ALU.add))
                choose(second, top2)
                v.tensor_tensor(both[:, :, :], first[:, :, :], second[:, :, :], ALU.add).then_inc(both_done, 1)
                v.tensor_tensor(top2[:, :], top2[:, :], top1[:, :], ALU.subtract).then_inc(gap_done, 1)
                dve.wait_ge(ratio_done, 1)
                then(v.tensor_scalar_add(den[:, :], ratio[:, :], 1.0))
                then(v.reciprocal(sh.weight[:, 0], den[:, :]))
                then(v.tensor_tensor(sh.weight[:, 1], ratio[:, :], sh.weight[:, 0], ALU.mult))
                dve.wait_ge(ranks_ready, 1)
                then(v.tensor_copy(scan[:, :, :].rearrange("p t e -> p (t e)"), tt[:, 0:NT * E]))
                a, b = scan, scan2
                for shift in (1, 2, 4):
                    v.tensor_copy(b[:, 0:shift], a[:, 0:shift])
                    then(v.tensor_tensor(b[:, shift:NT], a[:, shift:NT], a[:, 0:NT - shift], ALU.add))
                    a, b = b, a
                v.tensor_copy(rank[:, 0], rk[:, 0:E])
                then(v.tensor_tensor(rank[:, 1:NT].rearrange("p t e -> p (t e)"), rk[:, E:NT * E], a[:, 0:NT - 1].rearrange("p t e -> p (t e)"), ALU.add))
                load = a[:, NT - 1]
                then(v.scalar_tensor_tensor(more[:, :, :], load.unsqueeze(2).to_broadcast([P, E, more.shape[2]]), 1.0 / P,
                                            count_up[:, MINTILE:].unsqueeze(1).to_broadcast([P, E, more.shape[2]]), ALU.mult, ALU.is_gt))
                then(v.tensor_reduce(tiles[:, :], more[:, :, :], AX, ALU.add))
                then(v.tensor_scalar_add(tiles[:, :], tiles[:, :], float(MINTILE)))
                then(v.tensor_copy(start[:, :], tiles[:, :]))
                a, b = start, start2
                for shift in (1, 2, 4):
                    v.tensor_copy(b[:, 0:shift], a[:, 0:shift])
                    then(v.tensor_tensor(b[:, shift:E], a[:, shift:E], a[:, 0:E - shift], ALU.add))
                    a, b = b, a
                then(v.tensor_tensor(b[:, :], a[:, :], tiles[:, :], ALU.subtract))
                begin, end = b, a
                then(v.scalar_tensor_tensor(place[:, :, :], begin[:, :].unsqueeze(1).to_broadcast([P, NT, E]), float(P), rank[:, :, :], ALU.mult, ALU.add))
                for k, one_hot in enumerate((first, second)):
                    then(v.tensor_tensor(pick[:, :, :], place[:, :, :], one_hot[:, :, :], ALU.mult))
                    then(v.tensor_reduce(pos[:, k], pick[:, :, :], AX, ALU.add))
                v.tensor_copy(sh.pos[:, :, :], pos[:, :, :]).then_inc(pos_done, 1)
                v.tensor_copy(sh.table[:, 0], begin[:, :])
                v.tensor_scalar_add(sh.table[:, 1], tiles[:, :], -1.0)
                v.tensor_scalar_add(sh.table[:, 2], end[:, :], -1.0)
                for p in range(w.PIECES):
                    w.write_lo(dve, nc.vector, 0, p)


def expert_blocks(nc, A, sh):
    with ExitStack() as ctx:
        def sb(name, shape, dt=F32):
            return ctx.enter_context(nc.sbuf_tensor("f_" + name, shape, dt))

        def sem(name):
            return ctx.enter_context(nc.semaphore("f_" + name))

        w = sh.weights
        HALF, UP, PIECES, QH = w.HALF, w.UP, w.PIECES, w.HALF // P
        rows = sb("rows", [P, D])
        xT_hi, xT_lo = sb("xT_hi", [P, DCH, P], F32R), sb("xT_lo", [P, DCH, P], F32R)
        h = sb("h", [P, 2, HALF])
        hT_hi, hT_lo = sb("hT_hi", [P, 2, QH, P], F32R), sb("hT_lo", [P, 2, QH, P], F32R)
        y = sb("y", [P, D])
        up = [ctx.enter_context(nc.psum_tensor(f"f_up{n}", [P, BANK], F32)) for n in range(UP)]
        hT_bank = [ctx.enter_context(nc.psum_tensor(f"f_hT{n}", [P, BANK], F32)) for n in range(2)]
        y_bank, xT_bank = (ctx.enter_context(nc.psum_tensor(f"f_{n}_bank", [P, BANK], F32)) for n in ("y", "xT"))

        rows_in, xT_ready, xT_hi_done, xT_done = sem("rows_in"), sem("xT_ready"), sem("xT_hi_done"), sem("xT_done")
        used = sem("used")
        silu_done, h_done, hT_ready, hT_hi_done, hT_done = (sem(n) for n in ("silu_done", "h_done", "hT_ready", "hT_hi_done", "hT_done"))
        y_copied, y_out = sem("y_copied"), sem("y_out")
        waited = sem("waited")

        rows_d = sh.sorted_dram.rearrange("(t p) d -> t p d", p=P)
        y_d = sh.y_dram.rearrange("(t p) d -> t p d", p=P)

        def over_experts(eng, tile, peeled=1):
            def expert(e, following):
                def entry(n, low, high):
                    return eng.value_load(sh.table[0:1, n, bass.ds(e, 1)], min_val=low, max_val=high)

                first = entry(0, 0, MAXTILE - 1 - MINTILE)
                with eng.Fori(0, entry(1, MINTILE - 1, T // P - 1)) as k:
                    tile(eng.snap(first + k), e, False, False, False)
                tile(entry(2, MINTILE - 1, MAXTILE - 2), e, following >= 1, following == 0, following >= 2)

            with eng.Fori(0, E - peeled) as e:
                expert(e, peeled)
            for e in range(E - peeled, E):
                expert(e, E - 1 - e)

        with nc.Block() as block:
            @block.sync
            def _(sp):
                def tile(t, e, next_weights, final, loads):
                    if not final:
                        sp.wait_ge(xT_ready, t + 1)
                        sp.sem_inc(waited, 1)
                        sp.dma_start(rows[:, :], rows_d[(t + 1) & (MAXTILE - 1)]).then_inc(rows_in, 16)
                    if loads:
                        for p in range(PIECES):
                            w.wait_split(sp, e + 1, p)
                            sp.sem_inc(waited, 1)
                            w.load(sp, e + 2, p)
                    sp.wait_ge(y_copied, t + 2)
                    sp.sem_inc(waited, 1)
                    sp.dma_start(y_d[t & (MAXTILE - 1)], y[:, :]).then_inc(y_out, 16)

                sp.dma_start(rows[:, :], rows_d[0]).then_inc(rows_in, 16)
                for p in range(PIECES):
                    w.load(sp, 1, p)
                over_experts(sp, tile, peeled=2)
                last_tile = sp.value_load(sh.table[0:1, 2, E - 1:E], min_val=MINTILE - 1, max_val=MAXTILE - 2)
                sp.wait_ge(y_out, 16 * (last_tile + 2))
                sp.sem_inc(waited, 1)

            @block.scalar
            def _(act):
                def xT(t):
                    act.wait_ge(xT_ready, t + 1)
                    nc.scalar.copy(xT_hi[:, :, :], xT_bank[:, :].rearrange("p (c t) -> p c t", c=DCH)).then_inc(xT_hi_done, 1)

                def tile(t, e, next_weights, final, loads):
                    def silu(u):
                        act.wait_ge(used, PIECES * t + 2 * u + 1)
                        nc.scalar.activation(h[:, u], up[2 * u][:, :], ACT.Silu).then_inc(silu_done, 1)

                    def hT(u):
                        act.wait_ge(hT_ready, 2 * t + u + 1)
                        nc.scalar.copy(hT_hi[:, u], hT_bank[u][:, :].rearrange("p (q t) -> p q t", q=QH)).then_inc(hT_hi_done, 1)

                    def piece(p):
                        if next_weights:
                            act.wait_ge(used, PIECES * t + p + 1)
                            w.write_hi(act, e + 1, p)

                    silu(0)
                    piece(0)
                    piece(1)
                    silu(1)
                    hT(0)
                    piece(2)
                    piece(3)
                    hT(1)
                    if not final:
                        xT(t + 1)
                    piece(4)
                    piece(5)

                xT(0)
                over_experts(act, tile)

            @block.gpsimd
            def _(pool):
                with pool.Fori(0, E - 1) as e:
                    for p in range(w.BY_VECTOR, PIECES):
                        w.write_lo(pool, nc.gpsimd, e + 1, p)

            @block.vector
            def _(dve):
                def xT(t):
                    dve.wait_ge(xT_hi_done, t + 1)
                    split_lo(nc, xT_lo[:, :, :], xT_bank[:, :].rearrange("p (c t) -> p c t", c=DCH), xT_hi[:, :, :]).then_inc(xT_done, 1)

                def tile(t, e, next_weights, final, loads):
                    def gate(u):
                        dve.wait_ge(silu_done, 2 * t + u + 1)
                        dve.wait_ge(used, PIECES * t + 2 * u + 2)
                        nc.vector.tensor_tensor(h[:, u], up[2 * u + 1][:, :], h[:, u], ALU.mult).then_inc(h_done, 1)

                    def hT(u):
                        dve.wait_ge(hT_hi_done, 2 * t + u + 1)
                        split_lo(nc, hT_lo[:, u], hT_bank[u][:, :].rearrange("p (q t) -> p q t", q=QH), hT_hi[:, u]).then_inc(hT_done, 1)

                    def piece(p):
                        if next_weights:
                            w.write_lo(dve, nc.vector, e + 1, p)

                    gate(0)
                    piece(0)
                    hT(0)
                    piece(1)
                    gate(1)
                    hT(1)
                    piece(2)
                    if not final:
                        xT(t + 1)
                    piece(3)
                    dve.wait_ge(used, PIECES * t + PIECES)
                    dve.wait_ge(y_out, 16 * (t + 1))
                    nc.vector.tensor_copy(y[:, :], y_bank[:, :]).then_inc(y_copied, 1)
                    piece(4)

                dve.sem_inc(y_copied, 1)
                dve.sem_inc(y_out, 16)
                xT(0)
                over_experts(dve, tile)

            @block.tensor
            def _(pe):
                def xT(t):
                    pe.wait_ge(rows_in, 16 * (t + 1))
                    for c in range(DCH):
                        mm = nc.tensor.transpose(xT_bank[:, c * P:(c + 1) * P], rows[:, c * P:(c + 1) * P], sh.ident[:, :])
                    mm.then_inc(xT_ready, 1)

                def tile(t, e, next_weights, final, loads):
                    def up_product(p):
                        w.wait_split(pe, e, p)
                        for c in range(DCH):
                            at = slice(c * HALF, (c + 1) * HALF)
                            mm = three_passes(nc, up[p][:, :], xT_hi[:, c], xT_lo[:, c], w.hi[:, p, at], w.lo[:, p, at], c == 0, c == DCH - 1)
                        mm.then_inc(used, 1)

                    def hT(u):
                        pe.wait_ge(h_done, 2 * t + u + 1)
                        for q in range(QH):
                            mm = nc.tensor.transpose(hT_bank[u][:, q * P:(q + 1) * P], h[:, u, q * P:(q + 1) * P], sh.ident[:, :])
                        mm.then_inc(hT_ready, 1)

                    def down(u, q0, q1):
                        p = UP + u
                        if q0 == 0:
                            w.wait_split(pe, e, p)
                            pe.wait_ge(hT_done, 2 * t + u + 1)
                            if u == 0:
                                pe.wait_ge(y_copied, t + 1)
                        for q in range(q0, q1):
                            at = slice(q * D, (q + 1) * D)
                            mm = three_passes(nc, y_bank[:, :], hT_hi[:, u, q], hT_lo[:, u, q], w.hi[:, p, at], w.lo[:, p, at],
                                              u == 0 and q == 0, u == 1 and q == QH - 1)
                        if q1 == QH:
                            mm.then_inc(used, 1)

                    pe.wait_ge(xT_done, t + 1)
                    up_product(0)
                    up_product(1)
                    up_product(2)
                    hT(0)
                    up_product(3)
                    down(0, 0, QH // 2)
                    hT(1)
                    down(0, QH // 2, QH)
                    if not final:
                        xT(t + 1)
                    down(1, 0, QH)

                xT(0)
                over_experts(pe, tile)


def combine(nc, A, sh):
    with ExitStack() as ctx:
        got = ctx.enter_context(nc.sbuf_tensor("c_got", [P, NT, 2, D], F32))
        got_in = [ctx.enter_context(nc.semaphore(f"c_got_in{t}")) for t in range(NT)]
        half, done, stored = (ctx.enter_context(nc.semaphore(n)) for n in ("c_half", "c_done", "c_stored"))
        with nc.Block() as block:
            @block.gpsimd
            def _(pool):
                for t in range(NT):
                    for k in range(2):
                        pool.indirect_dma_start(got[:, t, k], None, sh.y_dram, bass.IndirectOffsetOnAxis(ap=sh.pos[:, k, t:t + 1], axis=0)).then_inc(got_in[t], 16)

            @block.vector
            def _(dve):
                for t in range(NT):
                    dve.wait_ge(got_in[t], 32)
                    for k in range(2):
                        ins = nc.vector.scalar_tensor_tensor(sh.x[:, t], got[:, t, k], sh.weight[:, k, t:t + 1], sh.x[:, t], ALU.mult, ALU.add)
                        if k == 0:
                            ins.then_inc(half, 1)
                            dve.wait_ge(half, t + 1)
                    ins.then_inc(done, 1)

            @block.sync
            def _(sp):
                out = A["out"].rearrange("b s d -> (b s) d").rearrange("(n p) d -> n p d", p=P)
                for t in range(NT):
                    sp.wait_ge(done, t + 1)
                    sp.dma_start(out[t], sh.x[:, t]).then_inc(stored, 16)
                sp.wait_ge(stored, 16 * NT)


def decoder_layer(nc, A):
    with ExitStack() as ctx:
        def sb(where, name, shape, dt=F32):
            return where.enter_context(nc.sbuf_tensor(name, shape, dt))

        sh = Shared()
        sh.last_dram = nc.dram_tensor("last_keys", (B, DC), F32, kind="Internal").ap()
        sh.ctx_dram = nc.dram_tensor("ctx_out", (NT, P, H * P), F32, kind="Internal").ap()
        sh.sorted_dram = nc.dram_tensor("sorted_rows", (MAXTILE * P, D), F32, kind="Internal").ap()
        sh.y_dram = nc.dram_tensor("expert_rows", (MAXTILE * P, D), F32, kind="Internal").ap()
        sh.ident = sb(ctx, "ident", [P, P])
        sh.ctx_tile = sb(ctx, "ctx_tile", [P, H, P])
        sh.ctx_stored = ctx.enter_context(nc.semaphore("ctx_stored"))
        with ExitStack() as cross:
            def pair(name, shape):
                return [sb(cross, f"{name}_{part}", shape, F32R) for part in ("hi", "lo")]

            sh.m1_hi, sh.m1_lo = pair("m1", [P, DCH, H * R])
            sh.xT_hi, sh.xT_lo = pair("xT", [P, DCH, T])
            sh.krT_hi, sh.krT_lo = pair("krT", [P, H, P])
            sh.lastT_hi, sh.lastT_lo = pair("lastT", [P, B])
            prepare(nc, A, sh)
            cross_attention(nc, A, sh)
        sh.x = sb(ctx, "x_res", [P, NT, D])
        sh.pos = sb(ctx, "pos", [P, 2, NT], I32)
        sh.weight = sb(ctx, "weight", [P, 2, NT])
        sh.table = sb(ctx, "table", [P, 3, E], I32)
        sh.self_norm, sh.route_norm = LayerNorm(nc, ctx, "s_ln"), LayerNorm(nc, ctx, "r_ln")
        project_context(nc, A, sh)
        self_attention(nc, A, sh)
        with ExitStack() as experts:
            sh.weights = ExpertWeights(nc, experts, A)
            route(nc, A, sh)
            expert_blocks(nc, A, sh)
        combine(nc, A, sh)


def shape_tables():
    f = np.float32
    inv = (f(1.0) / np.power(f(10000.0), np.arange(0, DC, 2, dtype=f) / f(DC))).astype(f)
    freqs = np.arange(L, dtype=f)[:, None] * inv[None, :]
    cos, sin = np.repeat(np.cos(freqs), 2, axis=-1).astype(f), np.repeat(np.sin(freqs), 2, axis=-1).astype(f)
    sin[:, :DC // 2] *= -1
    cut = {n: np.ascontiguousarray(t[:LC * P].reshape(LC, P, DC).transpose(1, 0, 2)) for n, t in (("cos", cos), ("sin", sin))}
    t, s = np.arange(S)[:, None], np.arange(S)[None, :]
    mask = np.tile(np.where((s <= t) & ((s < 4) | (s >= t - 64 + 1)), f(0), f(MASKED)).astype(f), (G, 1))
    before = (np.arange(P)[:, None] < np.arange(P)[None, :]).astype(f)
    return {
        "ident": np.eye(P, dtype=f), "cos": cut["cos"], "sin": cut["sin"],
        "last_cos": np.tile(cos[L - 1:], (B, 1)), "last_sin": np.tile(sin[L - 1:], (B, 1)),
        "mask": mask, "before": before,
        "order": np.tile(np.arange(E, 0, -1).astype(f), (P, 1)),
        "count_up": np.tile(np.arange(T // P).astype(f), (P, 1)),
    }


INPUTS = {"x": "x", "ctx_512": "ctx", "L0_xattn_Wq": "Wq", "L0_xattn_w_kc_q": "w_kc_q", "L0_xattn_w_kc_kv": "w_kc_kv",
          "L0_xattn_W_qr": "W_qr", "L0_xattn_W_kr": "W_kr", "L0_xattn_Wo": "Wo", "L0_attn_wq": "wq", "L0_attn_wk": "wk",
          "L0_attn_wv": "wv", "L0_attn_wo": "wo", "L0_ffn_gate_w": "gate_w", "L0_ffn_w0": "w0", "L0_ffn_w1": "w1",
          "L0_ffn_wo": "ffn_wo"}


def kernel(**inputs):
    import concourse.bacc as bacc
    from concourse.bass_utils import run_bass_kernel_spmd

    nc = bacc.Bacc("TRN2", target_bir_lowering=False, num_devices=1)
    arrays = {f"in_{short}": np.ascontiguousarray(inputs[name]) for name, short in INPUTS.items()}
    arrays |= {f"in_{name}": a for name, a in shape_tables().items()}
    A = {name[3:]: nc.dram_tensor(name, a.shape, mybir.dt.from_np(a.dtype), kind="ExternalInput").ap() for name, a in arrays.items()}
    A["out"] = nc.dram_tensor("out", (B, S, D), F32, kind="ExternalOutput").ap()
    decoder_layer(nc, A)
    return run_bass_kernel_spmd(nc, [arrays], core_ids=[0]).results[0]["out"]
```
